# Optimizing a Trainium2 kernel written in Bass

```python
import numpy as np
import jax
import jax.numpy as jnp

def _softmax(x, axis=-1):
    return jax.nn.softmax(x, axis=axis)

def _gelu(x):
    return jax.nn.gelu(x, approximate=True)

def _silu(x):
    return jax.nn.silu(x)

def _sigmoid(x):
    return jax.nn.sigmoid(x)

def _layernorm(x, axis=-1, eps=1e-05):
    m = jnp.mean(x, axis=axis, keepdims=True)
    v = jnp.var(x, axis=axis, keepdims=True)
    return (x - m) / jnp.sqrt(v + eps)

def _scatter_add(tgt, idx, src, axis=0):
    return tgt.at[idx].add(src)

def _segment_sum(src, seg, n):
    return jax.ops.segment_sum(src, seg, n)
kernel_name = 'mk_conv_preact_d4_conv_nhwc768_r4_266d65'

def setup_inputs(seed: int=0):
    np.random.seed(seed)
    _w = jnp.asarray

    def _rec_inputs():
        import jax
        import jax.numpy as jnp
        _gk = jax.random.key(seed)
        x = -0.0001538 + 1 * jax.random.normal(jax.random.fold_in(_gk, 1), (8, 32, 32, 192), jnp.float32)
        return x
    x = _rec_inputs()

    def _L0_conv_setup():
        import jax, jax.numpy as jnp
        import numpy as np
        NUM_HEADS = 12
        DIM = 192
        HEAD_DIM = DIM // NUM_HEADS
        SCALE = HEAD_DIM ** (-0.5)

        def _rot_half(t):
            d = t.shape[-1] // 2
            return jnp.concatenate([-t[..., d:], t[..., :d]], axis=-1)

        def _apply_rope_cat(t, rope):
            sin, cos = jnp.split(rope, 2, axis=-1)
            return t * cos + _rot_half(t) * sin
        key = jax.random.key(seed)
        ks = jax.random.split(key, 6)
        B, H, W = (8, 32, 32)
        x = jax.random.normal(ks[0], (B, H, W, DIM), dtype=jnp.float32)
        rope = jax.random.normal(ks[1], (H * W, 2 * HEAD_DIM), dtype=jnp.float32)
        qkv_w = jax.random.normal(ks[2], (DIM, 3 * DIM), dtype=jnp.float32) * DIM ** (-0.5)
        qkv_b = jax.random.normal(ks[3], (3 * DIM,), dtype=jnp.float32) * 0.02
        proj_w = jax.random.normal(ks[4], (DIM, DIM), dtype=jnp.float32) * DIM ** (-0.5)
        proj_b = jax.random.normal(ks[5], (DIM,), dtype=jnp.float32) * 0.02
        return {'x': x, 'rope': rope, 'qkv_w': qkv_w, 'qkv_b': qkv_b, 'proj_w': proj_w, 'proj_b': proj_b}
    _L0_conv_all = _L0_conv_setup()
    _L0_conv_in = {k: v for k, v in _L0_conv_all.items() if k in ('rope', 'qkv_w', 'qkv_b', 'proj_w', 'proj_b')}
    del _L0_conv_all

    def _L1_conv_setup():
        import jax, jax.numpy as jnp
        import numpy as np
        B_, H_, W_, DM = (4, 16, 16, 192)
        DI = int(0.5 * DM)
        N = 16
        R = -(-DM // 16)
        K = 4

        def selective_scan(xs, dts, As, Bs, Cs, Dsk):
            u = jnp.moveaxis(xs, -1, 0)
            d = jnp.moveaxis(dts, -1, 0)
            Bt = jnp.moveaxis(Bs, -1, 0)
            Ct = jnp.moveaxis(Cs, -1, 0)

            def step(h, inp):
                u_t, d_t, B_t, C_t = inp
                dA = jnp.exp(d_t[..., None] * As)
                h = h * dA + (d_t * u_t)[..., None] * B_t[:, :, None, :]
                y = jnp.einsum('bkcn,bkn->bkc', h, C_t)
                return (h, y)
            h0 = jnp.zeros(u.shape[1:] + (As.shape[-1],), u.dtype)
            _, ys = jax.lax.scan(step, h0, (u, d, Bt, Ct))
            ys = jnp.moveaxis(ys, 0, -1)
            return ys + Dsk[None, :, :, None] * xs
        key = jax.random.key(seed)
        ks = jax.random.split(key, 8)
        s = lambda i, shape, sc=0.02: jax.random.normal(ks[i], shape, jnp.float32) * sc
        return dict(x=jax.random.normal(ks[0], (B_, H_, W_, DM), jnp.float32), in_proj_w=s(1, (2 * DI, DM)), conv_w=s(2, (DI, 1, 3, 3)), conv_b=jnp.zeros((DI,), jnp.float32), x_proj_w=s(3, (K, R + 2 * N, DI)), dt_projs_w=s(4, (K, DI, R)), dt_projs_b=s(5, (K, DI)), A_logs=jnp.log(jnp.tile(jnp.arange(1, N + 1, dtype=jnp.float32)[None, :], (K * DI, 1))), Ds=jnp.ones((K * DI,), jnp.float32), out_norm_g=jnp.ones((DI,), jnp.float32), out_norm_b=jnp.zeros((DI,), jnp.float32), out_proj_w=s(6, (DM, DI)))
    _L1_conv_all = _L1_conv_setup()
    _L1_conv_in = {k: v for k, v in _L1_conv_all.items() if k in ('in_proj_w', 'conv_w', 'conv_b', 'x_proj_w', 'dt_projs_w', 'dt_projs_b', 'A_logs', 'Ds', 'out_norm_g', 'out_norm_b', 'out_proj_w')}
    del _L1_conv_all

    def _L2_conv_setup():
        import jax, jax.numpy as jnp
        import numpy as np
        B, H, W, C, NH = (100, 14, 14, 192, 12)
        HD = C // NH

        def _get_rel_pos(q_size, k_size, rel_pos):
            coords = jnp.arange(q_size)[:, None] - jnp.arange(k_size)[None, :] + (k_size - 1)
            return rel_pos[coords]
        key = jax.random.key(seed)
        ks = jax.random.split(key, 6)
        s = 0.02
        return {'hidden_states': jax.random.normal(ks[0], (B, H, W, C), jnp.float32), 'qkv_w': jax.random.normal(ks[1], (3 * C, C), jnp.float32) * s, 'qkv_b': jnp.zeros((3 * C,), jnp.float32), 'proj_w': jax.random.normal(ks[2], (C, C), jnp.float32) * s, 'proj_b': jnp.zeros((C,), jnp.float32), 'rel_pos_h': jax.random.normal(ks[3], (2 * H - 1, HD), jnp.float32) * s, 'rel_pos_w': jax.random.normal(ks[4], (2 * W - 1, HD), jnp.float32) * s}
    _L2_conv_all = _L2_conv_setup()
    _L2_conv_in = {k: v for k, v in _L2_conv_all.items() if k in ('qkv_w', 'qkv_b', 'proj_w', 'proj_b', 'rel_pos_h', 'rel_pos_w')}
    del _L2_conv_all

    def _L3_conv_setup():
        import jax, jax.numpy as jnp
        import numpy as np
        D_HEAD = 16
        KERNEL = 7

        def _neigh_idx(L, K):
            start = jnp.clip(jnp.arange(L) - K // 2, 0, L - K)
            return start[:, None] + jnp.arange(K)[None, :]
        key = jax.random.key(seed)
        k1, k2, k3 = jax.random.split(key, 3)
        B, H, W, D = (2, 48, 48, 192)
        x = jax.random.normal(k1, (B, H, W, D), jnp.float32)
        w_qkv = jax.random.normal(k2, (D, 3 * D), jnp.float32) / np.sqrt(D).astype(np.float32)
        w_out = jax.random.normal(k3, (D, D), jnp.float32) / np.sqrt(D).astype(np.float32)
        return {'x': x, 'w_qkv': w_qkv, 'w_out': w_out}
    _L3_conv_all = _L3_conv_setup()
    _L3_conv_in = {k: v for k, v in _L3_conv_all.items() if k in ('w_qkv', 'w_out')}
    del _L3_conv_all
    return {'x': x, 'L0_conv_rope': _L0_conv_in['rope'], 'L0_conv_qkv_w': _L0_conv_in['qkv_w'], 'L0_conv_qkv_b': _L0_conv_in['qkv_b'], 'L0_conv_proj_w': _L0_conv_in['proj_w'], 'L0_conv_proj_b': _L0_conv_in['proj_b'], 'L1_conv_in_proj_w': _L1_conv_in['in_proj_w'], 'L1_conv_conv_w': _L1_conv_in['conv_w'], 'L1_conv_conv_b': _L1_conv_in['conv_b'], 'L1_conv_x_proj_w': _L1_conv_in['x_proj_w'], 'L1_conv_dt_projs_w': _L1_conv_in['dt_projs_w'], 'L1_conv_dt_projs_b': _L1_conv_in['dt_projs_b'], 'L1_conv_A_logs': _L1_conv_in['A_logs'], 'L1_conv_Ds': _L1_conv_in['Ds'], 'L1_conv_out_norm_g': _L1_conv_in['out_norm_g'], 'L1_conv_out_norm_b': _L1_conv_in['out_norm_b'], 'L1_conv_out_proj_w': _L1_conv_in['out_proj_w'], 'L2_conv_qkv_w': _L2_conv_in['qkv_w'], 'L2_conv_qkv_b': _L2_conv_in['qkv_b'], 'L2_conv_proj_w': _L2_conv_in['proj_w'], 'L2_conv_proj_b': _L2_conv_in['proj_b'], 'L2_conv_rel_pos_h': _L2_conv_in['rel_pos_h'], 'L2_conv_rel_pos_w': _L2_conv_in['rel_pos_w'], 'L3_conv_w_qkv': _L3_conv_in['w_qkv'], 'L3_conv_w_out': _L3_conv_in['w_out']}

def reference(x, L0_conv_rope, L0_conv_qkv_w, L0_conv_qkv_b, L0_conv_proj_w, L0_conv_proj_b, L1_conv_in_proj_w, L1_conv_conv_w, L1_conv_conv_b, L1_conv_x_proj_w, L1_conv_dt_projs_w, L1_conv_dt_projs_b, L1_conv_A_logs, L1_conv_Ds, L1_conv_out_norm_g, L1_conv_out_norm_b, L1_conv_out_proj_w, L2_conv_qkv_w, L2_conv_qkv_b, L2_conv_proj_w, L2_conv_proj_b, L2_conv_rel_pos_h, L2_conv_rel_pos_w, L3_conv_w_qkv, L3_conv_w_out):
    import jax
    import jax.numpy as jnp

    def _L0_conv_ref(x, rope, qkv_w, qkv_b, proj_w, proj_b):
        import jax, jax.numpy as jnp
        import numpy as np
        NUM_HEADS = 12
        DIM = 192
        HEAD_DIM = DIM // NUM_HEADS
        SCALE = HEAD_DIM ** (-0.5)

        def _rot_half(t):
            d = t.shape[-1] // 2
            return jnp.concatenate([-t[..., d:], t[..., :d]], axis=-1)

        def _apply_rope_cat(t, rope):
            sin, cos = jnp.split(rope, 2, axis=-1)
            return t * cos + _rot_half(t) * sin
        B, H, W, C = x.shape
        N = H * W
        nh, hd = (NUM_HEADS, HEAD_DIM)
        qkv = jnp.einsum('bnc,cd->bnd', x.reshape(B, N, C), qkv_w) + qkv_b
        qkv = qkv.reshape(B, N, 3, nh, hd).transpose(2, 0, 3, 1, 4)
        q, k, v = (qkv[0], qkv[1], qkv[2])
        q = _apply_rope_cat(q, rope)
        k = _apply_rope_cat(k, rope)
        attn = jnp.einsum('bhqd,bhkd->bhqk', q * SCALE, k)
        attn = jax.nn.softmax(attn, axis=-1)
        out = jnp.einsum('bhqk,bhkd->bhqd', attn, v)
        out = out.transpose(0, 2, 1, 3).reshape(B, H, W, C)
        return jnp.einsum('bhwc,cd->bhwd', out, proj_w) + proj_b

    def _L1_conv_ref(x, in_proj_w, conv_w, conv_b, x_proj_w, dt_projs_w, dt_projs_b, A_logs, Ds, out_norm_g, out_norm_b, out_proj_w):
        import jax, jax.numpy as jnp
        import numpy as np
        B_, H_, W_, DM = (4, 16, 16, 192)
        DI = int(0.5 * DM)
        N = 16
        R = -(-DM // 16)
        K = 4

        def selective_scan(xs, dts, As, Bs, Cs, Dsk):
            u = jnp.moveaxis(xs, -1, 0)
            d = jnp.moveaxis(dts, -1, 0)
            Bt = jnp.moveaxis(Bs, -1, 0)
            Ct = jnp.moveaxis(Cs, -1, 0)

            def step(h, inp):
                u_t, d_t, B_t, C_t = inp
                dA = jnp.exp(d_t[..., None] * As)
                h = h * dA + (d_t * u_t)[..., None] * B_t[:, :, None, :]
                y = jnp.einsum('bkcn,bkn->bkc', h, C_t)
                return (h, y)
            h0 = jnp.zeros(u.shape[1:] + (As.shape[-1],), u.dtype)
            _, ys = jax.lax.scan(step, h0, (u, d, Bt, Ct))
            ys = jnp.moveaxis(ys, 0, -1)
            return ys + Dsk[None, :, :, None] * xs
        B, H, W, _ = x.shape
        L = H * W
        xz = x @ in_proj_w.T
        xh, z = jnp.split(xz, 2, axis=-1)
        xc = jnp.transpose(xh, (0, 3, 1, 2))
        xc = jax.lax.conv_general_dilated(xc, conv_w, (1, 1), 'SAME', feature_group_count=DI)
        xc = jax.nn.silu(xc + conv_b[None, :, None, None])
        x_flat = xc.reshape(B, DI, L)
        x_t = jnp.transpose(xc, (0, 1, 3, 2)).reshape(B, DI, L)
        x_hwwh = jnp.stack([x_flat, x_t], 1)
        xs = jnp.concatenate([x_hwwh, jnp.flip(x_hwwh, -1)], 1)
        x_dbl = jnp.einsum('bkdl,kcd->bkcl', xs, x_proj_w)
        dts, Bs, Cs = jnp.split(x_dbl, [R, R + N], axis=2)
        dts = jnp.einsum('bkrl,kdr->bkdl', dts, dt_projs_w)
        dts = jax.nn.softplus(dts + dt_projs_b[None, :, :, None])
        As = -jnp.exp(A_logs).reshape(K, DI, N)
        out_y = selective_scan(xs, dts, As, Bs, Cs, Ds.reshape(K, DI))
        inv_y = jnp.flip(out_y[:, 2:4], -1)
        wh_y = jnp.transpose(out_y[:, 1].reshape(B, DI, W, H), (0, 1, 3, 2)).reshape(B, DI, L)
        invwh_y = jnp.transpose(inv_y[:, 1].reshape(B, DI, W, H), (0, 1, 3, 2)).reshape(B, DI, L)
        y = out_y[:, 0] + inv_y[:, 0] + wh_y + invwh_y
        y = jnp.transpose(y, (0, 2, 1)).reshape(B, H, W, DI)
        mu = y.mean(-1, keepdims=True)
        var = y.var(-1, keepdims=True)
        y = (y - mu) / jnp.sqrt(var + 1e-05) * out_norm_g + out_norm_b
        y = y * jax.nn.silu(z)
        return y @ out_proj_w.T

    def _L2_conv_ref(hidden_states, qkv_w, qkv_b, proj_w, proj_b, rel_pos_h, rel_pos_w):
        import jax, jax.numpy as jnp
        import numpy as np
        B, H, W, C, NH = (100, 14, 14, 192, 12)
        HD = C // NH

        def _get_rel_pos(q_size, k_size, rel_pos):
            coords = jnp.arange(q_size)[:, None] - jnp.arange(k_size)[None, :] + (k_size - 1)
            return rel_pos[coords]
        b, h, w, c = hidden_states.shape
        scale = HD ** (-0.5)
        qkv = hidden_states.reshape(b, h * w, c) @ qkv_w.T + qkv_b
        qkv = qkv.reshape(b, h * w, 3, NH, HD).transpose(2, 0, 3, 1, 4)
        q, k, v = (qkv[0], qkv[1], qkv[2])
        Rh = _get_rel_pos(h, h, rel_pos_h)
        Rw = _get_rel_pos(w, w, rel_pos_w)
        qr = q.reshape(b, NH, h, w, HD)
        rel_h = jnp.einsum('bnhwc,hkc->bnhwk', qr, Rh)
        rel_w = jnp.einsum('bnhwc,wkc->bnhwk', qr, Rw)
        bias = (rel_h[..., :, None] + rel_w[..., None, :]).reshape(b, NH, h * w, h * w)
        attn = jnp.einsum('bnqd,bnkd->bnqk', q, k) * scale + bias
        attn = jax.nn.softmax(attn, axis=-1)
        out = jnp.einsum('bnqk,bnkd->bnqd', attn, v)
        out = out.transpose(0, 2, 1, 3).reshape(b, h, w, c)
        return out @ proj_w.T + proj_b

    def _L3_conv_ref(x, w_qkv, w_out):
        import jax, jax.numpy as jnp
        import numpy as np
        D_HEAD = 16
        KERNEL = 7

        def _neigh_idx(L, K):
            start = jnp.clip(jnp.arange(L) - K // 2, 0, L - K)
            return start[:, None] + jnp.arange(K)[None, :]
        B, H, W, D = x.shape
        e = D_HEAD
        nh = D // e
        K = KERNEL
        qkv = (x @ w_qkv).reshape(B, H, W, 3, nh, e)
        qkv = jnp.transpose(qkv, (3, 0, 4, 1, 2, 5))
        q, k, v = (qkv[0], qkv[1], qkv[2])
        q = q * e ** (-0.5)
        ih = _neigh_idx(H, K)
        iw = _neigh_idx(W, K)
        kg = k[:, :, ih[:, :, None, None], iw[None, None, :, :], :]
        scores = jnp.einsum('nhije,nhiajbe->nhijab', q, kg)
        attn = jax.nn.softmax(scores.reshape(B, nh, H, W, K * K), axis=-1)
        attn = attn.reshape(B, nh, H, W, K, K)
        vg = v[:, :, ih[:, :, None, None], iw[None, None, :, :], :]
        o = jnp.einsum('nhijab,nhiajbe->nhije', attn, vg)
        o = jnp.transpose(o, (0, 2, 3, 1, 4)).reshape(B, H, W, D)
        return o @ w_out

    def _gn(v, G=32, eps=1e-05):
        B_, H_, W_, C_ = v.shape
        g = v.reshape(B_, H_, W_, G, C_ // G)
        m = jnp.mean(g, axis=(1, 2, 4), keepdims=True)
        s = jnp.var(g, axis=(1, 2, 4), keepdims=True)
        return ((g - m) / jnp.sqrt(s + eps)).reshape(v.shape)

    def _ln_c(v, eps=1e-06):
        m = jnp.mean(v, axis=-1, keepdims=True)
        s = jnp.var(v, axis=-1, keepdims=True)
        return (v - m) / jnp.sqrt(s + eps)

    def _ln_t(v, eps=1e-05):
        m = jnp.mean(v, axis=-1, keepdims=True)
        s = jnp.var(v, axis=-1, keepdims=True)
        return (v - m) / jnp.sqrt(s + eps)

    def _to_tokens(v):
        B_, H_, W_, C_ = v.shape
        return v.reshape(B_, H_ * W_, C_)

    def _from_tokens(t, like):
        return t.reshape(like.shape)
    x = x + _L0_conv_ref(_gn(x), L0_conv_rope, L0_conv_qkv_w, L0_conv_qkv_b, L0_conv_proj_w, L0_conv_proj_b)
    x = x + _L1_conv_ref(_gn(x), L1_conv_in_proj_w, L1_conv_conv_w, L1_conv_conv_b, L1_conv_x_proj_w, L1_conv_dt_projs_w, L1_conv_dt_projs_b, L1_conv_A_logs, L1_conv_Ds, L1_conv_out_norm_g, L1_conv_out_norm_b, L1_conv_out_proj_w)
    x = x + _L2_conv_ref(_gn(x), L2_conv_qkv_w, L2_conv_qkv_b, L2_conv_proj_w, L2_conv_proj_b, L2_conv_rel_pos_h, L2_conv_rel_pos_w)
    x = x + _L3_conv_ref(_gn(x), L3_conv_w_qkv, L3_conv_w_out)
    return x

_drawn_inputs = setup_inputs


def setup_inputs(seed=0):
    import zlib

    import numpy as np

    out = dict(_drawn_inputs(seed))
    spreads = {'L1_conv_conv_b': (0.0, 0.1),
     'L1_conv_Ds': (1.0, 0.6),
     'L1_conv_out_norm_g': (1.0, 0.6),
     'L1_conv_out_norm_b': (0.0, 0.8),
     'L2_conv_qkv_b': (0.0, 0.1),
     'L2_conv_proj_b': (0.0, 0.1)}
    factors = {'L1_conv_conv_w': 8.0,
     'L1_conv_x_proj_w': 64.0,
     'L1_conv_dt_projs_w': 64.0,
     'L1_conv_dt_projs_b': 200.0,
     'L1_conv_A_logs': 200.0,
     'L2_conv_qkv_w': 8.0,
     'L2_conv_rel_pos_h': 8.0,
     'L2_conv_rel_pos_w': 8.0}
    for name, (base, spread) in spreads.items():
        noise = np.random.default_rng([zlib.crc32(name.encode()), seed]).standard_normal(out[name].shape)
        drawn = base * np.exp(spread * noise) if base else spread * noise
        out[name] = jnp.asarray(drawn.astype(out[name].dtype))
    for name, factor in factors.items():
        out[name] = (out[name] * factor).astype(out[name].dtype)
    return out
```

```python
from contextlib import ExitStack

import numpy as np

import concourse.bass as bass
from concourse import mybir

F32 = mybir.dt.float32
F32R = mybir.dt.float32r
ALU = mybir.AluOpType
ACT = mybir.ActivationFunctionType
AX = mybir.AxisListType

B, H, W, C = 8, 32, 32, 192
N = H * W
NH, HD = 12, 16
CP = 96
NC = C // CP
P = 128
NT = N // P
HF = 512
NHF = N // HF
NBUF = 3
TURNS = NH // NBUF
QR = 3 * HD
MR = 2
GROUP = 6
A_LOG_MAX = 84.0
CONSTANTS = 41
KD, NS, R = 4, 16, 12
DB = P // NS
NG = CP // DB
WIN = 7
KROWS = 10
HEAD_IN = {"A": 6 * 16, "C": 6 * 16, "D": 7 * 16}
BIG = -1.0e30
FR = P // W



def constants():
    c = {}
    c["ident"] = np.eye(P, dtype=np.float32)
    ch = np.arange(CP)
    c["group"] = ((ch[:, None] // GROUP == ch[None, :] // GROUP) / GROUP).astype(np.float32)
    c["mean"] = np.full((CP, CP), 1.0 / CP, np.float32)
    rot = np.zeros((CP, CP), np.float32)
    for j in range(CP):
        d = j % HD
        if d < HD // 2:
            rot[j + HD // 2, j] = -1.0
        else:
            rot[j - HD // 2, j] = 1.0
    c["rot"] = rot
    tok = np.arange(N)
    hot = np.concatenate([np.arange(H)[:, None] == tok[None, :] // W,
                          np.arange(W)[:, None] == tok[None, :] % W]).astype(np.float32)
    c["onehot"] = np.concatenate([hot, hot])
    start = np.clip(np.arange(H) - WIN // 2, 0, H - WIN)
    seen = (np.arange(H)[:, None] >= start[None, :]) & (np.arange(H)[:, None] < start[None, :] + WIN)
    far = np.where(seen, 0.0, BIG).astype(np.float32)
    c["window"] = np.concatenate([far[:, tok // W], far[:, tok % W]]).astype(np.float32)
    p = np.arange(P)
    spread = np.zeros((CP, NG, P), np.float32)
    for g in range(NG):
        spread[DB * g + p // NS, g, p] = 1.0
    c["spread"] = spread
    c["gather"] = np.ascontiguousarray(spread.transpose(2, 1, 0))
    lo = np.zeros((QR, 1), np.float32)
    lo[HD:2 * HD] = -1.0
    c["lorows"] = lo
    c["spread"] = np.concatenate([c["spread"], c["spread"][:, 0:2]], axis=1)
    c["gather"] = np.concatenate([c["gather"], c["gather"][:, 0:2]], axis=1)
    return c



ATTN = ("A", "C", "D")
BIASED = ("A", "C")


class Space:
    pass


class NormSignals:
    def __init__(self, sem, L):
        self.stats = sem(f"{L}_stats")
        self.stat_sums = sem(f"{L}_stat_sums")
        self.var = sem(f"{L}_var")
        self.rstd = sem(f"{L}_rstd")
        self.xn = sem(f"{L}_xn")


class AttentionSignals(NormSignals):
    def __init__(self, sem, L):
        NormSignals.__init__(self, sem, L)
        self.qk_ps = sem(f"{L}_qk_ps")
        self.raw = sem(f"{L}_raw")
        self.rot_ps = sem(f"{L}_rot_ps")
        self.split = sem(f"{L}_split")
        self.v_ps = sem(f"{L}_v_ps")
        self.v_used = sem(f"{L}_v_used")
        self.s_ps = sem(f"{L}_s_ps")
        self.mx_used = sem(f"{L}_mx_used")
        self.mx = sem(f"{L}_mx")
        self.mt = sem(f"{L}_mt")
        self.nm = sem(f"{L}_nm")
        self.nm_in = sem(f"{L}_nm_in")
        self.st_ps = sem(f"{L}_st_ps")
        self.pt = sem(f"{L}_pt")
        self.pt_used = sem(f"{L}_pt_used")
        self.o_used = sem(f"{L}_o_used")
        self.ot_ps = sem(f"{L}_ot_ps")
        self.ocm = sem(f"{L}_ocm")
        self.proj_ps = sem(f"{L}_proj_ps")
        self.x_done = sem(f"{L}_x_done")
        self.rq_ps = sem(f"{L}_rq_ps")
        self.rq_hi = sem(f"{L}_rq_hi")
        self.rq = sem(f"{L}_rq")
        self.stored = [sem(f"{L}_stored{i}") for i in range(2)]
        self.heads = [sem(f"{L}_heads{i}") for i in range(NBUF)]


class ScanSignals(NormSignals):
    def __init__(self, sem, L):
        NormSignals.__init__(self, sem, L)
        self.xz_ps = sem(f"{L}_xz_ps")
        self.xh = sem(f"{L}_xh")
        self.z = sem(f"{L}_z")
        self.u_conv = sem(f"{L}_u_conv")
        self.u_exp = sem(f"{L}_u_exp")
        self.u = sem(f"{L}_u")
        self.dtr_ps = sem(f"{L}_dtr_ps")
        self.dtr = sem(f"{L}_dtr")
        self.dtp_ps = sem(f"{L}_dtp_ps")
        self.v = sem(f"{L}_v")
        self.e = sem(f"{L}_e")
        self.dt_split = sem(f"{L}_dt_split")
        self.brep_ps = sem(f"{L}_brep_ps")
        self.brep = sem(f"{L}_brep")
        self.crep_ps = sem(f"{L}_crep_ps")
        self.crep = sem(f"{L}_crep")
        self.sel = sem(f"{L}_sel")
        self.dtb_ps = sem(f"{L}_dtb_ps")
        self.da = sem(f"{L}_da")
        self.dub_ps = sem(f"{L}_dub_ps")
        self.bt = sem(f"{L}_bt")
        self.h = sem(f"{L}_h")
        self.hc = sem(f"{L}_hc")
        self.y_used = sem(f"{L}_y_used")
        self.ysb = sem(f"{L}_ysb")
        self.mean_ps = sem(f"{L}_mean_ps")
        self.sq = sem(f"{L}_sq")
        self.var_ps = sem(f"{L}_var_ps")
        self.rln = sem(f"{L}_rln")
        self.yz = sem(f"{L}_yz")
        self.out_ps = sem(f"{L}_out_ps")
        self.x_done = sem(f"{L}_x_done")


def allocate(nc, ctx):
    m = Space()

    def sb(stack, name, shape, dt=F32):
        return stack.enter_context(nc.sbuf_tensor(name, shape, dt))

    def ps(name, shape):
        return ctx.enter_context(nc.psum_tensor(name, shape, F32))

    m.s1 = ps("s1", [P, 2, HF])
    m.s2 = ps("s2", [P, 2, N])
    m.px = ps("px", [P, 2, HF])

    m.x = sb(ctx, "x", [CP, NC, N])
    m.xn = sb(ctx, "xn", [CP, NC, N])
    m.gn = sb(ctx, "gn", [CP, NC, 2, 6])
    m.mv = sb(ctx, "mv", [CP, NC, 2])
    m.gs = sb(ctx, "gs", [CP, NC, 2])
    m.gt = sb(ctx, "gt", [CP, NC])
    m.gv = sb(ctx, "gv", [CP, NC])
    m.gl = sb(ctx, "gl", [CP, NC])
    m.gr = sb(ctx, "gr", [CP, NC])
    m.eps = sb(ctx, "eps", [CP, 1])
    m.ident = sb(ctx, "ident", [P, P])
    m.group = sb(ctx, "group", [CP, CP])
    m.mean = sb(ctx, "mean", [CP, CP])
    m.rot = sb(ctx, "rot", [CP, CP])
    m.qs = [sb(ctx, f"qs{i}", [P, N], F32R) for i in range(NBUF)]
    m.ks = [sb(ctx, f"ks{i}", [P, N], F32R) for i in range(NBUF)]
    m.hot = sb(ctx, "hot", [P, N], F32R)
    m.v1 = sb(ctx, "v1", [P, NT, NH, HD + 1])
    m.w = {}
    for L in ATTN:
        m.w[L] = Space()
        m.w[L].qkv = sb(ctx, f"qkv_w{L}", [CP, NC, 3 * C])
        m.w[L].proj = sb(ctx, f"proj_w{L}", [CP, NC, C])
        if L in BIASED:
            m.w[L].qkb = sb(ctx, f"qk_b{L}", [CP, 4])
            m.w[L].vb = sb(ctx, f"v_b{L}", [P, 2, NH, HD])
            m.w[L].pb = sb(ctx, f"proj_b{L}", [CP, NC])
    m.relh = sb(ctx, "relh", [QR, H, H], F32R)
    m.relw = sb(ctx, "relw", [QR, W, W], F32R)
    m.inw = sb(ctx, "inw", [CP, NC, C])
    m.outw = sb(ctx, "outw", [CP, C])
    m.convw = sb(ctx, "convw", [CP, 9])
    m.convb = sb(ctx, "convb", [CP, 1])
    m.xdtw = sb(ctx, "xdtw", [CP, KD, R])
    m.xbw = sb(ctx, "xbw", [CP, KD, P])
    m.xcw = sb(ctx, "xcw", [CP, KD, P])
    m.dtw = sb(ctx, "dtw", [R, KD, CP])
    m.dtb = sb(ctx, "dtb", [CP, KD])
    m.arow = sb(ctx, "arow", [P, KD * NG])
    m.dskip = sb(ctx, "dskip", [CP, KD])
    m.diag = sb(ctx, "diag", [CP, CP])
    m.spread_t = sb(ctx, "spread_t", [CP, NG + 2, P], F32R)
    m.gather_t = sb(ctx, "gather_t", [P, NG + 2, CP])
    m.spread = sb(ctx, "spread", [CP, 4, P], F32R)
    m.gather = sb(ctx, "gather", [P, 4, CP])
    m.lorows = sb(ctx, "lorows", [QR, 1])
    m.lng = sb(ctx, "lng", [CP, 1])
    m.lnb = sb(ctx, "lnb", [CP, 1])

    with ExitStack() as attn:
        m.cos = sb(attn, "cos", [CP, N])
        m.sin = sb(attn, "sin", [CP, N])
        m.raw = [sb(attn, f"raw{i}", [CP, N]) for i in range(2)]
        m.ra = sb(attn, "ra", [CP, N])
        m.rb = sb(attn, "rb", [CP, N])
        m.hi = [sb(attn, f"hi{i}", [CP, N], F32R) for i in range(2)]
        m.lo = [sb(attn, f"lo{i}", [CP, N], F32R) for i in range(2)]
        m.pt = [sb(attn, f"pt{i}", [P, N]) for i in range(4)]
        m.rq = [sb(attn, f"rq{i}", [P, N], F32R) for i in range(NBUF)]
        m.mxp = sb(attn, "mxp", [P, NT, NHF])
        m.mx = sb(attn, "mx", [P, NT])
        m.nm = sb(attn, "nm", [NT, MR, P], F32R)
        m.rc = sb(attn, "rc", [P, NT])
        m.otok = sb(attn, "otok", [P, NT, C])
        m.ocm = sb(attn, "ocm", [CP, NC, N])
    with ExitStack() as scan:
        m.pad = sb(scan, "pad", [CP, H + 2, W + 2])
        m.zs = sb(scan, "zs", [CP, N])
        m.u = sb(scan, "u", [CP, 2, N])
        m.t0 = sb(scan, "t0", [CP, N])
        m.t1 = sb(scan, "t1", [CP, N])
        m.dtr = sb(scan, "dtr", [R, N])
        m.dt = sb(scan, "dt", [CP, N])
        m.du = sb(scan, "du", [CP, N])
        m.dth = sb(scan, "dth", [CP, 2, N], F32R)
        m.duh = sb(scan, "duh", [CP, 2, N], F32R)
        m.brep = sb(scan, "brep", [P, N])
        m.crep = sb(scan, "crep", [P, N])
        m.da = [sb(scan, f"da{i}", [P, N]) for i in range(2)]
        m.bt = [sb(scan, f"bt{i}", [P, N]) for i in range(2)]
        m.hs = [sb(scan, f"hs{i}", [P, N]) for i in range(2)]
        m.z = m.hs[0][0:CP]
        m.hc = [sb(scan, f"hc{i}", [P, N]) for i in range(2)]

    m.qd = nc.dram_tensor("q_split", (2, C, N), F32, kind="Internal").ap()
    m.kd = nc.dram_tensor("k_split", (2, C, N), F32, kind="Internal").ap()

    m.zero = nc.dram_tensor("zero_rows", (MR, N), F32, kind="Internal").ap()

    def sem(name):
        return ctx.enter_context(nc.semaphore(name))

    m.const_in = sem("const_in")
    m.const_ready = sem("const_ready")
    m.a_log = sem("a_log")
    m.zero_in = sem("zero_in")
    m.a_exp = sem("a_exp")
    m.x_in = sem("x_in")
    m.rope_in = sem("rope_in")
    m.settled = sem("settled")
    m.out_done = sem("out_done")
    m.s = {L: AttentionSignals(sem, L) for L in ATTN}
    m.s["B"] = ScanSignals(sem, "B")
    return m



def norm_vector(nc, dve, m, L, b):
    s = m.s[L]
    for c in range(NC):
        for f in range(NHF):
            nc.vector.bn_stats(m.gn[:, c, f, :], m.x[:, c, f * HF:(f + 1) * HF])
    nc.vector.drain()
    for c in range(NC):
        nc.vector.bn_aggr(m.mv[:, c, :], m.gn[:, c, :, :])
    nc.vector.drain()
    nc.vector.tensor_tensor(m.gt[:], m.mv[:, :, 0], m.mv[:, :, 0], ALU.mult)
    nc.vector.drain()
    nc.vector.tensor_tensor(m.mv[:, :, 1], m.mv[:, :, 1], m.gt[:], ALU.add).then_inc(s.stats, 1)
    dve.wait_ge(s.stat_sums, b + 1)
    nc.vector.tensor_copy(m.gs[:], m.px[0:CP, 1, 0:2 * NC].rearrange("p (c s) -> p c s", c=NC))
    nc.vector.drain()
    nc.vector.tensor_tensor(m.gt[:], m.gs[:, :, 0], m.gs[:, :, 0], ALU.mult)
    nc.vector.drain()
    nc.vector.tensor_tensor(m.gv[:], m.gs[:, :, 1], m.gt[:], ALU.subtract).then_inc(s.var, 1)
    dve.wait_ge(s.rstd, b + 1)
    for c in range(NC):
        nc.vector.tensor_scalar(m.xn[:, c, :], m.x[:, c, :], m.gs[:, c, 0:1], m.gr[:, c:c + 1],
                                ALU.subtract, ALU.mult).then_inc(s.xn, 1)


def norm_scalar(nc, act, m, L, b):
    s = m.s[L]
    act.wait_ge(s.var, b + 1)
    nc.scalar.activation(m.gl[:], m.gv[:], ACT.Ln, bias=m.eps[:, 0:1])
    nc.scalar.drain()
    nc.scalar.activation(m.gr[:], m.gl[:], ACT.Exp, scale=-0.5).then_inc(s.rstd, 1)


def norm_tensor(nc, pe, m, L, b):
    s = m.s[L]
    pe.wait_ge(s.stats, b + 1)
    nc.tensor.matmul(m.px[0:CP, 1, 0:2 * NC], m.group[:], m.mv[:].rearrange("p c s -> p (c s)"),
                     start=True, stop=True).then_inc(s.stat_sums, 1)



def spans(L):
    if L == "D":
        keys = [(W * min(max(FR * t - WIN // 2, 0), H - KROWS), W * KROWS) for t in range(NT)]
        queries = [(P * min(max(t - 1, 0), NT - 3), 3 * P) for t in range(NT)]
    else:
        keys = queries = [(0, N)] * NT
    return keys, queries


def tiles_of(L, t):
    return [q for q in range(NT) if L != "D" or abs(q - t) <= 1]


def pieces(L):
    keys, _ = spans(L)
    return [(t, k0 + o, min(HF, n)) for t, (k0, n) in enumerate(keys) for o in range(0, n, HF)]


def by_image(m, axis):
    rows = m.s1[0:H, :, :].rearrange("p a n -> p (a n)")
    return rows.rearrange("p (c r) -> p r c", r=H) if axis else rows.rearrange("p (r c) -> p r c", r=H)


JOBS = [(0, 0), (1, 0), (0, 1), (1, 1)]


def heads_loop(eng, body):
    with eng.Fori(0, TURNS - 1) as j:
        for u in range(NBUF):
            body(j, u, True)
    for u in range(NBUF):
        body(TURNS - 1, u, u + 1 < NBUF)


def settle(eng, m):
    eng.sem_inc(m.settled, 1)


def following(j, u):
    return (j + 1, 0) if u == NBUF - 1 else (j, u + 1)


def attn_tensor(nc, pe, m, L, b):
    s, w = m.s[L], m.w[L]
    keys, queries = spans(L)
    norm_tensor(nc, pe, m, L, b)
    pe.wait_ge(s.xn, NC * b + NC)
    for i, (which, c) in enumerate(JOBS):
        if i >= 2:
            pe.wait_ge(s.raw, 4 * b + i - 1)
        for f in range(NHF):
            for kc in range(NC):
                last = nc.tensor.matmul(
                    m.s2[0:CP, i % 2, f * HF:(f + 1) * HF],
                    w.qkv[:, kc, which * C + c * CP:which * C + (c + 1) * CP],
                    m.xn[:, kc, f * HF:(f + 1) * HF], start=kc == 0, stop=kc == NC - 1)
        last.then_inc(s.qk_ps, 1)
        if L == "A":
            pe.wait_ge(s.raw, 4 * b + i + 1)
            if i >= 1:
                pe.wait_ge(s.split, 4 * b + i)
            for f in range(NHF):
                last = nc.tensor.matmul(m.s1[0:CP, f, :], m.rot[:], m.raw[i % 2][:, f * HF:(f + 1) * HF],
                                        start=True, stop=True)
            last.then_inc(s.rot_ps, 1)
    if L == "A":
        pe.wait_ge(s.split, 4 * b + 4)
    for i in range(NT // 2):
        if i >= 2:
            pe.wait_ge(s.v_used, 4 * b + i - 1)
        for a in range(2):
            t = 2 * i + a
            for kc in range(NC):
                last = nc.tensor.matmul(m.s1[:, i % 2, a * C:(a + 1) * C], m.xn[:, kc, t * P:(t + 1) * P],
                                        w.qkv[:, kc, 2 * C:3 * C], start=kc == 0, stop=kc == NC - 1)
        last.then_inc(s.v_ps, 1)
    pe.wait_ge(s.v_used, 4 * b + 4)
    pe.wait_ge(s.raw, 4 * b + 4)

    todo = pieces(L)
    per = len(todo)

    def relative(h, u, axis):
        pe.wait_ge(s.mx_used, NH * per * b + per * h + 1)
        if axis:
            pe.wait_ge(s.rq, 2 * (NH * b + h) + 1)
        settle(pe, m)
        table = (m.relh, m.relw)[axis]
        for r in range(H):
            q = m.qs[u][0:QR, r:N:W] if axis else m.qs[u][0:QR, r * W:(r + 1) * W]
            last = nc.tensor.matmul(m.s1[0:H, r * W // HF, (r * W) % HF:(r * W) % HF + W], table[:, r, :], q,
                                    start=True, stop=True)
        last.then_inc(s.rq_ps, 1)

    def first(j, u, i):
        h = j * NBUF + u
        t, k0, n = todo[i]
        out = m.s1[:, i % 2, 0:n]
        q = slice(t * P, (t + 1) * P)
        fresh = isinstance(h, int) and h == 0 and i == 0
        if L == "C" and i == 0:
            pe.wait_ge(s.rq, 2 * (NH * b + h) + 2)
        if not fresh and (i >= 2 or L != "C"):
            pe.wait_ge(s.mx_used, NH * per * b + per * h + i)
        rows = P if L == "D" else QR
        last = nc.tensor.matmul(out, m.qs[u][0:rows, q], m.ks[u][0:rows, k0:k0 + n], start=True, stop=L != "C")
        if L == "C":
            last = nc.tensor.matmul(out, m.rq[u][:, q], m.hot[:, k0:k0 + n], start=False, stop=True)
        last.then_inc(s.s_ps, 1)

    def begin(j, u):
        h = j * NBUF + u
        pe.wait_ge(s.heads[u], HEAD_IN[L] * (TURNS * b + j + 1))
        if L == "C":
            relative(h, u, 0)

    def maxima(h):
        pe.wait_ge(s.mx, NH * b + h + 1)
        nc.tensor.transpose(m.px[0:NT, 1, 0:P], m.mx[:], m.ident[:]).then_inc(s.mt, 1)

    def second(h, u, t):
        q0, n = queries[t]
        k = slice(t * P, (t + 1) * P)
        if t == 0:
            pe.wait_ge(s.nm_in, 16 * MR * (NH * b + h + 1))
        pe.wait_ge(s.pt, NH * NT * b + NT * h + t + 1)
        rows = P if L == "D" else QR + MR
        for f0 in range(0, n, HF):
            nf = min(HF, n - f0)
            out = m.s2[:, t % 2, f0:f0 + nf]
            last = nc.tensor.matmul(out, m.ks[u][0:rows, k], m.qs[u][0:rows, q0 + f0:q0 + f0 + nf],
                                    start=True, stop=L != "C")
            if L == "C":
                last = nc.tensor.matmul(out, m.hot[:, k], m.rq[u][:, q0 + f0:q0 + f0 + nf],
                                        start=False, stop=True)
        last.then_inc(s.st_ps, 1)

    def values(h, t):
        q0, _ = queries[t]
        pe.wait_ge(s.pt, NH * NT * b + NT * h + t + 3)
        if t == 0:
            pe.wait_ge(s.o_used, NH * b + h + 1)
        for q in tiles_of(L, t):
            last = nc.tensor.matmul(m.px[:, 0, q * (HD + 1):(q + 1) * (HD + 1)],
                                    m.pt[t % 4][:, q * P - q0:(q + 1) * P - q0],
                                    m.v1[:, t, bass.ds(h, 1), :].rearrange("p a d -> p (a d)"),
                                    start=t == 0 and q == 0, stop=t == NT - 1, skip_group_check=True)
        last.then_inc(s.pt_used, 1)

    def body(j, u, more):
        h = j * NBUF + u
        nj, nu = following(j, u)
        if more:
            begin(nj, nu)
        for t in range(NT):
            second(h, u, t)
            if more and L == "C" and t == 0:
                relative(nj * NBUF + nu, nu, 1)
            lag = 1 if L == "C" else 0
            if more and lag <= t < lag + 4:
                for i in range((t - lag) * per // 4, (t - lag + 1) * per // 4):
                    first(nj, nu, i)
            if t >= 1:
                values(h, t - 1)
            if more and t == 6:
                maxima(nj * NBUF + nu)
        values(h, NT - 1)

    begin(0, 0)
    if L == "C":
        relative(0, 0, 1)
    for i in range(per):
        first(0, 0, i)
    maxima(0)
    heads_loop(pe, body)
    pe.wait_ge(s.o_used, NH * b + NH + 1)
    pe.wait_ge(s.pt, NH * NT * (b + 1) + 2)
    for c in range(NC):
        for t in range(NT):
            last = nc.tensor.transpose(m.s2[0:CP, c, t * P:(t + 1) * P], m.otok[:, t, c * CP:(c + 1) * CP],
                                       m.ident[:])
        last.then_inc(s.ot_ps, 1)
    pe.wait_ge(s.ocm, NC * b + NC)
    for c in range(NC):
        for f in range(NHF):
            for kc in range(NC):
                out = m.s1[0:CP, f, :] if c == 0 else m.s2[0:CP, 0, f * HF:(f + 1) * HF]
                last = nc.tensor.matmul(out, w.proj[:, kc, c * CP:(c + 1) * CP],
                                        m.ocm[:, kc, f * HF:(f + 1) * HF], start=kc == 0, stop=kc == NC - 1)
        last.then_inc(s.proj_ps, 1)


def attn_scalar(nc, act, m, L, b):
    s, w = m.s[L], m.w[L]
    _, queries = spans(L)
    norm_scalar(nc, act, m, L, b)
    for i, (which, c) in enumerate(JOBS):
        act.wait_ge(s.qk_ps, 4 * b + i + 1)
        if i >= 2:
            act.wait_ge(s.split, 4 * b + i - 1)
        scale = HD ** -0.5 if L == "C" and which == 1 else 1.0
        if L in BIASED:
            nc.scalar.activation(m.raw[i % 2][:], m.s2[0:CP, i % 2, :], ACT.Identity,
                                 bias=w.qkb[:, 2 * which + c:2 * which + c + 1], scale=scale).then_inc(s.raw, 1)
        else:
            nc.scalar.activation(m.raw[i % 2][:], m.s2[0:CP, i % 2, :], ACT.Copy).then_inc(s.raw, 1)

    def relative(h, u, axis):
        act.wait_ge(s.rq_ps, 2 * (NH * b + h) + axis + 1)
        nc.scalar.activation(m.rq[u][axis * H:(axis + 1) * H, :].rearrange("p (r c) -> p r c", r=H),
                             by_image(m, axis), ACT.Copy).then_inc(s.rq_hi, 1)

    def body(j, u, more):
        h = j * NBUF + u
        if more and L == "C":
            nj, nu = following(j, u)
            relative(nj * NBUF + nu, nu, 0)
        for t in range(NT):
            if more and L == "C" and t == 1:
                relative(nj * NBUF + nu, nu, 1)
            n = queries[t][1]
            act.wait_ge(s.st_ps, NH * NT * b + NT * h + t + 1)
            act.wait_ge(s.pt_used, NH * NT * b + NT * h + t + 1)
            nc.scalar.activation(m.pt[t % 4][:, 0:n], m.s2[:, t % 2, 0:n], ACT.Exp,
                                 scale=1.0 if L == "C" else HD ** -0.5).then_inc(s.pt, 1)

    if L == "C":
        relative(0, 0, 0)
        relative(0, 0, 1)
    heads_loop(act, body)
    for c in range(NC):
        act.wait_ge(s.ot_ps, NC * b + c + 1)
        nc.scalar.activation(m.ocm[:, c, :], m.s2[0:CP, c, :], ACT.Copy).then_inc(s.ocm, 1)


def attn_vector(nc, dve, m, L, b):
    s, w = m.s[L], m.w[L]
    norm_vector(nc, dve, m, L, b)
    if L == "A":
        dve.wait_ge(m.rope_in, 32 * b + 32)
    for i, (which, c) in enumerate(JOBS):
        dve.wait_ge(s.raw, 4 * b + i + 1)
        src = m.raw[i % 2]
        if L == "A":
            nc.vector.tensor_tensor(m.ra[:], src[:], m.cos[:], ALU.mult)
            dve.wait_ge(s.rot_ps, 4 * b + i + 1)
            nc.vector.tensor_tensor(m.rb[:], m.s1[0:CP, :, :].rearrange("p a n -> p (a n)"), m.sin[:], ALU.mult)
            nc.vector.drain()
            nc.vector.tensor_tensor(src[:], m.ra[:], m.rb[:], ALU.add)
            nc.vector.drain()
        if i >= 2:
            dve.wait_ge(s.stored[i % 2], 64 * b + 32)
        nc.vector.tensor_copy(m.hi[i % 2][:], src[:])
        nc.vector.drain()
        nc.vector.tensor_tensor(m.lo[i % 2][:], src[:], m.hi[i % 2][:].bitcast(F32), ALU.subtract) \
            .then_inc(s.split, 1)
    for i in range(NT // 2):
        dve.wait_ge(s.v_ps, 4 * b + i + 1)
        for a in range(2):
            dst = m.v1[:, 2 * i + a, :, 0:HD]
            psum = m.s1[:, i % 2, a * C:(a + 1) * C].rearrange("p (h d) -> p h d", h=NH)
            if L in BIASED:
                last = nc.vector.tensor_tensor(dst, psum, w.vb[:, a, :, :], ALU.add)
            else:
                last = nc.vector.tensor_copy(dst, psum)
        last.then_inc(s.v_used, 1)

    todo = pieces(L)
    per = len(todo)
    halves = per // NT

    def relative(h, u):
        for axis in range(2):
            dve.wait_ge(s.rq_hi, 2 * (NH * b + h) + axis + 1)
            hi = m.rq[u][axis * H:(axis + 1) * H, :].bitcast(F32).rearrange("p (r c) -> p r c", r=H)
            lo = m.rq[u][(axis + 2) * H:(axis + 3) * H, :].rearrange("p (r c) -> p r c", r=H)
            nc.vector.tensor_tensor(lo, by_image(m, axis), hi, ALU.subtract).then_inc(s.rq, 1)

    def first(h, u):
        for i, (t, _, n) in enumerate(todo):
            dve.wait_ge(s.s_ps, NH * per * b + per * h + i + 1)
            out = m.mxp[:, t, i % 2:i % 2 + 1] if halves == 2 else m.mx[:, t:t + 1]
            last = nc.vector.tensor_reduce(out, m.s1[:, i % 2, 0:n], AX.X, ALU.max).then_inc(s.mx_used, 1)
        if halves == 2:
            nc.vector.drain()
            nc.vector.tensor_reduce(m.mx[:], m.mxp[:], AX.X, ALU.max)
        nc.vector.drain().then_inc(s.mx, 1)
        dve.wait_ge(s.mt, NH * b + h + 1)
        nc.vector.tensor_scalar(m.nm[:, 0, :], m.px[0:NT, 1, 0:P], -1.0, None, ALU.mult)
        nc.vector.drain()
        nc.vector.scalar_tensor_tensor(m.nm[:, 1, :], m.px[0:NT, 1, 0:P], -1.0, m.nm[:, 0, :].bitcast(F32),
                                       ALU.mult, ALU.subtract).then_inc(s.nm, 1)

    def finish(h):
        dve.wait_ge(s.pt_used, NH * NT * b + NT * h + NT + 4)
        o = m.px[:, 0, 0:NT * (HD + 1)].rearrange("p (t d) -> p t d", d=HD + 1)
        nc.vector.reciprocal(m.rc[:], o[:, :, HD])
        nc.vector.drain()
        nc.vector.tensor_tensor(m.otok[:, :, bass.ds(h * HD, HD)], o[:, :, 0:HD],
                                m.rc[:, :, None].broadcast_to([P, NT, HD]), ALU.mult).then_inc(s.o_used, 1)

    def body(j, u, more):
        if more:
            nj, nu = following(j, u)
            if L == "C":
                relative(nj * NBUF + nu, nu)
            first(nj * NBUF + nu, nu)
        finish(j * NBUF + u)

    if L == "C":
        relative(0, 0)
    first(0, 0)
    heads_loop(dve, body)
    for c in range(NC):
        dve.wait_ge(s.proj_ps, NC * b + c + 1)
        psum = m.s1[0:CP, :, :].rearrange("p a n -> p (a n)") if c == 0 else m.s2[0:CP, 0, :]
        if L in BIASED:
            nc.vector.scalar_tensor_tensor(m.x[:, c, :], psum, w.pb[:, c:c + 1], m.x[:, c, :],
                                           ALU.add, ALU.add).then_inc(s.x_done, 1)
        else:
            nc.vector.tensor_tensor(m.x[:, c, :], psum, m.x[:, c, :], ALU.add).then_inc(s.x_done, 1)
    nc.vector.drain()


def attn_sync(nc, sp, m, L, b):
    s = m.s[L]
    for i, (which, c) in enumerate(JOBS):
        sp.wait_ge(s.split, 4 * b + i + 1)
        dst = m.kd if which else m.qd
        for part, src in enumerate((m.hi, m.lo)):
            sp.dma_start(dst[part, c * CP:(c + 1) * CP, :], src[i % 2][:].bitcast(F32)) \
                .then_inc(s.stored[i % 2], 16)
    for i in range(2):
        sp.wait_ge(s.stored[i], 64 * b + 64)

    def load(j, u):
        row = (j * NBUF + u) * HD
        for dst, src, order in ((m.qs[u], m.qd, (0, 0, 1)), (m.ks[u], m.kd, (0, 1, 0))):
            for r, part in enumerate(order):
                sp.dma_start(dst[r * HD:(r + 1) * HD, :].bitcast(F32), src[part, bass.ds(row, HD), :]) \
                    .then_inc(s.heads[u], 16)

        if L == "D":
            sp.dma_start(m.qs[u][QR:QR + MR, :].bitcast(F32), m.zero).then_inc(s.heads[u], 16)

    def maxima(h, u):
        sp.wait_ge(s.nm, NH * b + h + 1)
        for r in range(MR):
            sp.dma_start(m.qs[u][QR + r:QR + r + 1, :].bitcast(F32).rearrange("r (t n) -> r t n", t=NT),
                         m.nm[:, r, :].bitcast(F32)).then_inc(s.nm_in, 16)

    def body(j, u, more):
        h = j * NBUF + u
        if more:
            nj, nu = following(j, u)
            maxima(nj * NBUF + nu, nu)
        if not isinstance(j, int):
            sp.wait_ge(s.st_ps, NH * NT * b + NT * h + NT)
            settle(sp, m)
            load(j + 1, u)

    for u in range(NBUF):
        load(0, u)
    maxima(0, 0)
    heads_loop(sp, body)



TILES = KD * NG


def scan_order(ap, k):
    return ap[:, ::-1] if k >= 2 else ap


def scan_tensor(nc, pe, m, b):
    s = m.s["B"]
    norm_tensor(nc, pe, m, "B", b)
    pe.wait_ge(s.xn, NC * b + NC)
    for o in range(2):
        for f in range(NHF):
            for kc in range(NC):
                last = nc.tensor.matmul(m.s2[0:CP, o, f * HF:(f + 1) * HF], m.inw[:, kc, o * CP:(o + 1) * CP],
                                        m.xn[:, kc, f * HF:(f + 1) * HF], start=kc == 0, stop=kc == NC - 1)
        last.then_inc(s.xz_ps, 1)
    pe.wait_ge(s.u, b + 1)
    for f in range(NHF):
        nc.tensor.matmul(m.px[0:CP, f, :], m.diag[:], m.u[:, 0, f * HF:(f + 1) * HF],
                         start=True, stop=False, skip_group_check=True)

    def tile(k, g, v):
        i = TILES * b + NG * k + g
        pe.wait_ge(s.sel, i + 1)
        pe.wait_ge(s.da, i + 1)
        for f in range(NHF):
            for part in range(2):
                last = nc.tensor.matmul(m.s1[:, f, :], m.spread[:, v, :], m.dth[:, part, f * HF:(f + 1) * HF],
                                        start=part == 0, stop=part == 1)
        last.then_inc(s.dtb_ps, 1)
        pe.wait_ge(s.bt, i + 1)
        for f in range(NHF):
            for part in range(2):
                last = nc.tensor.matmul(m.s2[:, v % 2, f * HF:(f + 1) * HF], m.spread[:, v, :],
                                        m.duh[:, part, f * HF:(f + 1) * HF], start=part == 0, stop=part == 1)
        last.then_inc(s.dub_ps, 1)

    def total(k, g, v):
        i = TILES * b + NG * k + g
        pe.wait_ge(s.hc, i + 3)
        hc = scan_order(m.hc[v % 2], k)
        for f in range(NHF):
            if k % 2 == 0:
                rhs = hc[:, f * HF:(f + 1) * HF]
            else:
                rhs = hc.rearrange("p (w h) -> p h w", h=H)[:, f * H // 2:(f + 1) * H // 2, :]
            last = nc.tensor.matmul(m.px[0:CP, f, :], m.gather[:, v, :], rhs, start=False,
                                    stop=k == KD - 1, skip_group_check=True)
        last.then_inc(s.y_used, 1)

    for k in range(KD):
        turn = KD * b + k
        uk = scan_order(m.u[:, k % 2, :], k)
        pe.wait_ge(s.da, TILES * b + NG * k + 1)
        for f in range(NHF):
            last = nc.tensor.matmul(m.s1[0:R, f, :], m.xdtw[:, k, :], uk[:, f * HF:(f + 1) * HF],
                                    start=True, stop=True)
        last.then_inc(s.dtr_ps, 1)
        pe.wait_ge(s.bt, TILES * b + NG * k + 2)
        for o, (wt, ready) in enumerate(((m.xbw, s.brep_ps), (m.xcw, s.crep_ps))):
            for f in range(NHF):
                last = nc.tensor.matmul(m.s2[:, o, f * HF:(f + 1) * HF], wt[:, k, :],
                                        uk[:, f * HF:(f + 1) * HF], start=True, stop=True)
            last.then_inc(ready, 1)
            if o == 0:
                pe.wait_ge(s.dtr, turn + 1)
                for f in range(NHF):
                    last = nc.tensor.matmul(m.s1[0:CP, f, :], m.dtw[:, k, :], m.dtr[:, f * HF:(f + 1) * HF],
                                            start=True, stop=True)
                last.then_inc(s.dtp_ps, 1)
        pe.wait_ge(s.crep, turn + 1)
        pe.wait_ge(s.dt_split, turn + 1)
        for v in range(4):
            tile(k, v, v)
            if v >= 2:
                total(k, v - 2, v - 2)
        with pe.Fori(1, NG // 4) as q:
            for v in range(4):
                tile(k, q * 4 + v, v)
                total(k, q * 4 + v - 2, (v - 2) % 4)
        for g in (NG - 2, NG - 1):
            total(k, g, g % 4)
    pe.wait_ge(s.ysb, b + 1)
    for f in range(NHF):
        last = nc.tensor.matmul(m.s1[0:CP, f, :], m.mean[:], m.t0[:, f * HF:(f + 1) * HF], start=True, stop=True)
    last.then_inc(s.mean_ps, 1)
    pe.wait_ge(s.sq, b + 1)
    for f in range(NHF):
        last = nc.tensor.matmul(m.s2[0:CP, 0, f * HF:(f + 1) * HF], m.mean[:], m.dt[:, f * HF:(f + 1) * HF],
                                start=True, stop=True)
    last.then_inc(s.var_ps, 1)
    pe.wait_ge(s.yz, b + 1)
    for c in range(NC):
        for f in range(NHF):
            out = m.s1[0:CP, f, :] if c == 0 else m.s2[0:CP, 1, f * HF:(f + 1) * HF]
            last = nc.tensor.matmul(out, m.outw[:, c * CP:(c + 1) * CP], m.du[:, f * HF:(f + 1) * HF],
                                    start=True, stop=True)
        last.then_inc(s.out_ps, 1)


def scan_scalar(nc, act, m, b):
    s = m.s["B"]
    norm_scalar(nc, act, m, "B", b)
    act.wait_ge(s.xz_ps, 2 * b + 1)
    nc.scalar.activation(m.pad[:, 1:H + 1, 1:W + 1], m.s2[0:CP, 0, :].rearrange("p (h w) -> p h w", h=H),
                         ACT.Copy).then_inc(s.xh, 1)
    act.wait_ge(s.xz_ps, 2 * b + 2)
    nc.scalar.activation(m.z, m.s2[0:CP, 1, :], ACT.Copy)
    nc.scalar.activation(m.zs[:], m.s2[0:CP, 1, :], ACT.Exp, scale=-1.0).then_inc(s.z, 1)
    act.wait_ge(s.u_conv, b + 1)
    nc.scalar.activation(m.t1[:], m.t0[:], ACT.Exp, scale=-1.0).then_inc(s.u_exp, 1)
    s1 = m.s1[:].rearrange("p a n -> p (a n)")

    def tile(k, g, v):
        i = TILES * b + NG * k + g
        act.wait_ge(s.dtb_ps, i + 1)
        act.wait_ge(s.h, i + 1)
        nc.scalar.activation(m.da[v % 2][:], s1, ACT.Exp,
                             scale=m.arow[:, bass.ds(NG * k + g, 1)]).then_inc(s.da, 1)

    for k in range(KD):
        turn = KD * b + k
        act.wait_ge(s.dtr_ps, turn + 1)
        nc.scalar.activation(m.dtr[:], s1[0:R, :], ACT.Copy).then_inc(s.dtr, 1)
        act.wait_ge(s.brep_ps, turn + 1)
        nc.scalar.activation(m.brep[:], m.s2[:, 0, :], ACT.Copy).then_inc(s.brep, 1)
        act.wait_ge(s.v, turn + 1)
        nc.scalar.activation(m.t1[:], m.t1[:], ACT.Exp)
        nc.scalar.drain()
        nc.scalar.activation(m.dt[:], m.t1[:], ACT.Copy, bias=1.0)
        nc.scalar.drain()
        nc.scalar.activation(m.du[:], m.dt[:], ACT.Ln).then_inc(s.e, 1)
        act.wait_ge(s.crep_ps, turn + 1)
        nc.scalar.activation(m.crep[:], m.s2[:, 1, :], ACT.Copy).then_inc(s.crep, 1)
        with act.Fori(0, NG // 4) as q:
            for v in range(4):
                tile(k, q * 4 + v, v)
    act.wait_ge(s.var_ps, b + 1)
    nc.scalar.activation(m.t0[:], m.s2[0:CP, 0, :], ACT.Ln, bias=m.eps[:, 0:1])
    nc.scalar.drain()
    nc.scalar.activation(m.t0[:], m.t0[:], ACT.Exp, scale=-0.5).then_inc(s.rln, 1)


def scan_vector(nc, dve, m, b):
    s = m.s["B"]
    norm_vector(nc, dve, m, "B", b)
    s1 = m.s1[0:CP, :, :].rearrange("p a n -> p (a n)")
    nc.vector.memset(m.pad[:, 0, :], 0.0)
    nc.vector.memset(m.pad[:, H + 1, :], 0.0)
    nc.vector.memset(m.pad[:, 1:H + 1, 0:1], 0.0)
    nc.vector.memset(m.pad[:, 1:H + 1, W + 1:W + 2], 0.0)
    nc.vector.drain()
    dve.wait_ge(s.xh, b + 1)
    acc = m.t0[:].rearrange("p (h w) -> p h w", h=H)
    nc.vector.tensor_scalar(acc, m.pad[:, 0:H, 0:W], m.convw[:, 0:1], m.convb[:, 0:1], ALU.mult, ALU.add)
    for a in range(1, 9):
        nc.vector.drain()
        last = nc.vector.scalar_tensor_tensor(acc, m.pad[:, a // 3:a // 3 + H, a % 3:a % 3 + W],
                                              m.convw[:, a:a + 1], acc, ALU.mult, ALU.add)
    last.then_inc(s.u_conv, 1)
    dve.wait_ge(s.z, b + 1)
    nc.vector.tensor_scalar(m.zs[:], m.zs[:], 1.0, None, ALU.add)
    nc.vector.drain()
    nc.vector.reciprocal(m.zs[:], m.zs[:])
    nc.vector.drain()
    nc.vector.tensor_tensor(m.zs[:], m.zs[:], m.z, ALU.mult)
    dve.wait_ge(s.u_exp, b + 1)
    nc.vector.tensor_scalar(m.t1[:], m.t1[:], 1.0, None, ALU.add)
    nc.vector.drain()
    nc.vector.reciprocal(m.t1[:], m.t1[:])
    nc.vector.drain()
    nc.vector.tensor_tensor(m.u[:, 0, :], m.t0[:], m.t1[:], ALU.mult)
    nc.vector.drain()
    nc.vector.tensor_copy(m.u[:, 1, :].rearrange("p (w h) -> p w h", h=H),
                          m.u[:, 0, :].rearrange("p (h w) -> p w h", h=H)).then_inc(s.u, 1)

    def tile(k, g, v):
        i = TILES * b + NG * k + g
        dve.wait_ge(s.dub_ps, i + 1)
        nc.vector.tensor_tensor(m.bt[v % 2][:], m.s2[:, v % 2, :], m.brep[:], ALU.mult).then_inc(s.bt, 1)
        nc.vector.drain()
        dve.wait_ge(s.da, i + 2)
        dve.wait_ge(s.hc, i + 1)
        nc.vector.tensor_tensor_scan(m.hs[v % 2][:], m.da[v % 2][:], m.bt[v % 2][:], 0.0,
                                     ALU.mult, ALU.add).then_inc(s.h, 1)

    for k in range(KD):
        turn = KD * b + k
        dve.wait_ge(s.dtp_ps, turn + 1)
        nc.vector.tensor_scalar(m.t0[:], s1, m.dtb[:, k:k + 1], None, ALU.add)
        nc.vector.drain()
        nc.vector.scalar_tensor_tensor(m.t1[:], m.t0[:], -1.0, m.t0[:], ALU.mult, ALU.min).then_inc(s.v, 1)
        dve.wait_ge(s.e, turn + 1)
        nc.vector.scalar_tensor_tensor(m.dt[:], m.dt[:], 1.0, m.t1[:], ALU.subtract, ALU.subtract)
        nc.vector.drain()
        nc.vector.tensor_tensor(m.du[:], m.du[:], m.dt[:], ALU.subtract)
        nc.vector.drain()
        nc.vector.scalar_tensor_tensor(m.du[:], m.t1[:], 0.5, m.du[:], ALU.mult, ALU.max)
        nc.vector.drain()
        nc.vector.scalar_tensor_tensor(m.dt[:], m.t0[:], 0.0, m.du[:], ALU.max, ALU.add)
        nc.vector.drain()
        nc.vector.tensor_tensor(m.du[:], m.dt[:], scan_order(m.u[:, k % 2, :], k), ALU.mult)
        nc.vector.tensor_copy(m.dth[:, 0, :], m.dt[:])
        nc.vector.drain()
        nc.vector.tensor_copy(m.duh[:, 0, :], m.du[:])
        nc.vector.tensor_tensor(m.dth[:, 1, :], m.dt[:], m.dth[:, 0, :].bitcast(F32), ALU.subtract)
        nc.vector.drain()
        nc.vector.tensor_tensor(m.duh[:, 1, :], m.du[:], m.duh[:, 0, :].bitcast(F32), ALU.subtract) \
            .then_inc(s.dt_split, 1)
        dve.wait_ge(s.brep, turn + 1)
        settle(dve, m)
        with dve.Fori(0, NG // 4) as q:
            for v in range(4):
                tile(k, q * 4 + v, v)
    dve.wait_ge(s.y_used, TILES * b + TILES + 4)
    nc.vector.tensor_copy(m.t0[:], m.px[0:CP, :, :].rearrange("p a n -> p (a n)")).then_inc(s.ysb, 1)
    nc.vector.drain()
    dve.wait_ge(s.mean_ps, b + 1)
    nc.vector.tensor_tensor(m.t1[:], m.t0[:], s1, ALU.subtract)
    nc.vector.drain()
    nc.vector.tensor_tensor(m.dt[:], m.t1[:], m.t1[:], ALU.mult).then_inc(s.sq, 1)
    dve.wait_ge(s.rln, b + 1)
    nc.vector.tensor_tensor(m.t1[:], m.t1[:], m.t0[:], ALU.mult)
    nc.vector.drain()
    nc.vector.tensor_scalar(m.t1[:], m.t1[:], m.lng[:, 0:1], m.lnb[:, 0:1], ALU.mult, ALU.add)
    nc.vector.drain()
    nc.vector.tensor_tensor(m.du[:], m.t1[:], m.zs[:], ALU.mult).then_inc(s.yz, 1)
    for c in range(NC):
        dve.wait_ge(s.out_ps, NC * b + c + 1)
        psum = s1 if c == 0 else m.s2[0:CP, 1, :]
        nc.vector.tensor_tensor(m.x[:, c, :], psum, m.x[:, c, :], ALU.add).then_inc(s.x_done, 1)
    nc.vector.drain()


def place_selectors(nc, pool, m, i, g, v):
    s = m.s["B"]
    pool.wait_ge(s.y_used, i + 1)
    nc.gpsimd.tensor_copy(m.gather[:, v, :], m.gather_t[:, bass.ds(g, 1), :].rearrange("p a n -> p (a n)"))
    nc.gpsimd.tensor_copy(m.spread[:, v, :], m.spread_t[:, bass.ds(g, 1), :].rearrange("p a n -> p (a n)")
                          .bitcast(F32)).then_inc(s.sel, 1)


def scan_pool(nc, pool, m, b):
    s = m.s["B"]
    for k in range(KD):
        pool.wait_ge(s.crep, KD * b + k + 1)
        settle(pool, m)
        with pool.Fori(0, NG // 4) as q:
            for v in range(4):
                i = TILES * b + NG * k + q * 4 + v
                place_selectors(nc, pool, m, i + 2, q * 4 + v + 2, (v + 2) % 4)
                pool.wait_ge(s.h, i + 3)
                pool.wait_ge(s.y_used, i + 3)
                nc.gpsimd.tensor_tensor(m.hc[v % 2][:], m.hs[v % 2][:], m.crep[:], ALU.mult).then_inc(s.hc, 1)



def build(nc, d, out):
    ctx = ExitStack()
    nc.disable_value_cache = True
    with ctx:
        m = allocate(nc, ctx)
        block = ctx.enter_context(nc.Block())

        @block.sync
        def _(sp):
            loads = [(m.ident[:], d["ident"]), (m.group[:], d["group"]), (m.mean[:], d["mean"]),
                     (m.rot[:], d["rot"]),
                     (m.pt[0][:], d["onehot"]), (m.pt[1][64:P, :], d["window"]),
                     (m.lorows[:], d["lorows"]), (m.gather_t[:], d["gather"]),
                     (m.otok[0:CP].rearrange("p t c -> p (t c)")[:, 0:1024], d["spread"][:, 0:8, :]),
                     (m.inw[:], d["in_w"]), (m.outw[:], d["out_w"]), (m.convw[:], d["conv_w"]),
                     (m.convb[:], d["conv_b"]), (m.xdtw[:], d["xdt_w"]), (m.xbw[:], d["xb_w"]),
                     (m.xcw[:], d["xc_w"]), (m.dtw[:], d["dt_w"]), (m.dtb[:], d["dt_b"]),
                     (m.arow[:], d["a_log"]), (m.dskip[:], d["d_skip"]), (m.lng[:], d["ln_g"]),
                     (m.lnb[:], d["ln_b"])]
            loads[8] = (m.raw[0][:].rearrange("p (g n) -> p g n", n=P), d["spread"][:, 0:8, :])
            loads.append((m.raw[1][:, 0:(NG - 6) * P].rearrange("p (g n) -> p g n", n=P), d["spread"][:, 8:, :]))
            for L in ATTN:
                loads += [(m.w[L].qkv[:], d[f"qkv_w{L}"]), (m.w[L].proj[:], d[f"proj_w{L}"])]
                if L in BIASED:
                    vb = d[f"qkv_b{L}"]
                    loads += [(m.w[L].qkb[:], d[f"qk_b{L}"]), (m.w[L].pb[:], d[f"proj_b{L}"]),
                              (m.w[L].vb[:].rearrange("p a h d -> p a (h d)"),
                               bass.AP(vb.tensor, 2 * C, [[0, P], [0, 2], [1, C]]))]
            for i in range(2):
                loads += [(m.ocm[r * HD:(r + 1) * HD, i, :].rearrange("p (q k) -> p q k", k=H),
                           d[("rel_h", "rel_w")[i]]) for r in range(3)]
            for dst, src in loads:
                sp.dma_start(dst, src).then_inc(m.const_in, 16)
            assert len(loads) == CONSTANTS
            sp.wait_ge(m.a_log, 1)
            sp.dma_start(m.zero, m.ra[0:MR, :]).then_inc(m.zero_in, 16)
            sp.wait_ge(m.const_ready, 1)
            sp.wait_ge(m.zero_in, 16)
            with sp.Fori(0, B) as b:
                sp.dma_start(m.x[:], d["x"][bass.ds(b, 1)].rearrange("a c p n -> p (a c) n")) \
                    .then_inc(m.x_in, 16)
                sp.dma_start(m.cos[:], d["cos"]).then_inc(m.rope_in, 16)
                sp.dma_start(m.sin[:], d["sin"]).then_inc(m.rope_in, 16)
                for L in ATTN:
                    attn_sync(nc, sp, m, L, b)
                sp.wait_ge(m.s["D"].x_done, NC * b + NC)
                sp.dma_start(out[bass.ds(b, 1)].rearrange("a c p n -> p (a c) n"), m.x[:]) \
                    .then_inc(m.out_done, 16)
                sp.wait_ge(m.out_done, 16 * b + 16)
                settle(sp, m)

        @block.vector
        def _(dve):
            nc.vector.memset(m.ra[0:MR, :], 0.0).then_inc(m.a_log, 1)
            nc.vector.memset(m.eps[:], 1e-5)
            nc.vector.memset(m.v1[:, :, :, HD:HD + 1], 1.0)
            for u in range(NBUF):
                nc.vector.memset(m.qs[u][32:64, :].bitcast(F32), 0.0)
                nc.vector.memset(m.ks[u][32:64, :].bitcast(F32), 1.0)
            dve.wait_ge(m.const_in, 16 * CONSTANTS)
            nc.vector.tensor_scalar(m.arow[:], m.arow[:], A_LOG_MAX, None, ALU.min).then_inc(m.a_log, 1)
            nc.vector.tensor_copy(m.hot[:], m.pt[0][:])
            for u in range(NBUF):
                nc.vector.tensor_copy(m.qs[u][64:P, :], m.pt[1][64:P, :])
                nc.vector.tensor_copy(m.ks[u][64:P, :], m.pt[0][64:P, :])
            nc.vector.tensor_copy(m.spread_t[:, 0:8, :], m.raw[0][:].rearrange("p (g n) -> p g n", n=P))
            nc.vector.tensor_copy(m.spread_t[:, 8:, :], m.raw[1][:, 0:(NG - 6) * P].rearrange("p (g n) -> p g n", n=P))
            nc.vector.tensor_scalar(m.w["C"].qkb[:, 2:4], m.w["C"].qkb[:, 2:4], HD ** -0.5, None, ALU.mult)
            nc.vector.tensor_reduce(m.gt[:, 0:1], m.dskip[:], AX.X, ALU.add)
            nc.vector.drain()
            nc.vector.tensor_scalar(m.diag[:], m.ident[0:CP, 0:CP], m.gt[:, 0:1], None, ALU.mult)
            dve.wait_ge(m.a_exp, 1)
            nc.vector.tensor_scalar(m.arow[:], m.arow[:], -1.0, None, ALU.mult)
            for i, rel in enumerate((m.relh, m.relw)):
                v = m.ocm[0:QR, i, :].rearrange("p (q k) -> p q k", k=H)
                nc.vector.tensor_copy(rel[:], v)
                nc.vector.drain()
                nc.vector.scalar_tensor_tensor(rel[:], rel[:].bitcast(F32), m.lorows[:, 0:1], v,
                                               ALU.mult, ALU.add)
            nc.vector.drain().then_inc(m.const_ready, 1)
            with dve.Fori(0, B) as b:
                dve.wait_ge(m.x_in, 16 * b + 16)
                attn_vector(nc, dve, m, "A", b)
                scan_vector(nc, dve, m, b)
                attn_vector(nc, dve, m, "C", b)
                attn_vector(nc, dve, m, "D", b)

        @block.scalar
        def _(act):
            for L in ATTN:
                act.sem_inc(m.s[L].pt, 2)
            act.sem_inc(m.s["B"].da, 1)
            act.wait_ge(m.a_log, 2)
            nc.scalar.activation(m.arow[:], m.arow[:], ACT.Exp).then_inc(m.a_exp, 1)
            act.wait_ge(m.const_ready, 1)
            with act.Fori(0, B) as b:
                attn_scalar(nc, act, m, "A", b)
                scan_scalar(nc, act, m, b)
                attn_scalar(nc, act, m, "C", b)
                attn_scalar(nc, act, m, "D", b)

        @block.tensor
        def _(pe):
            for L in ATTN:
                pe.sem_inc(m.s[L].pt_used, 4)
                pe.sem_inc(m.s[L].mx_used, 1)
                pe.sem_inc(m.s[L].o_used, 1)
            pe.sem_inc(m.s["B"].bt, 2)
            pe.sem_inc(m.s["B"].h, 2)
            pe.sem_inc(m.s["B"].y_used, 4)
            pe.wait_ge(m.const_ready, 1)
            with pe.Fori(0, B) as b:
                attn_tensor(nc, pe, m, "A", b)
                scan_tensor(nc, pe, m, b)
                attn_tensor(nc, pe, m, "C", b)
                attn_tensor(nc, pe, m, "D", b)

        @block.gpsimd
        def _(pool):
            pool.sem_inc(m.s["B"].hc, 2)
            pool.wait_ge(m.const_ready, 1)
            for g in range(2):
                place_selectors(nc, pool, m, g, g, g)
            with pool.Fori(0, B) as b:
                scan_pool(nc, pool, m, b)



def chunks(a):
    return a.reshape(NC, CP, -1).transpose(1, 0, 2)


def layout(i):
    d = dict(constants())
    d["x"] = i["x"].reshape(B, N, NC, CP).transpose(0, 2, 3, 1)
    rope = i["L0_conv_rope"].reshape(N, 2, HD).transpose(1, 2, 0)
    d["sin"], d["cos"] = np.tile(rope[0], (CP // HD, 1)), np.tile(rope[1], (CP // HD, 1))
    d["qkv_wA"], d["proj_wA"] = chunks(i["L0_conv_qkv_w"]), chunks(i["L0_conv_proj_w"])
    d["qkv_wC"], d["proj_wC"] = chunks(i["L2_conv_qkv_w"].T), chunks(i["L2_conv_proj_w"].T)
    d["qkv_wD"], d["proj_wD"] = chunks(i["L3_conv_w_qkv"]), chunks(i["L3_conv_w_out"])
    for L, n in (("A", "L0"), ("C", "L2")):
        qkv_b = i[f"{n}_conv_qkv_b"]
        d[f"qkv_b{L}"] = qkv_b
        d[f"qk_b{L}"] = qkv_b[0:2 * C].reshape(4, CP).T
        d[f"proj_b{L}"] = i[f"{n}_conv_proj_b"].reshape(NC, CP).T
    at = np.arange(H)[:, None] - np.arange(H)[None, :] + H - 1
    for n in ("h", "w"):
        table = i[f"L2_conv_rel_pos_{n}"]
        d[f"rel_{n}"] = table[np.minimum(at, table.shape[0] - 1)].transpose(2, 0, 1)
    d["in_w"] = chunks(i["L1_conv_in_proj_w"].T)
    d["out_w"] = i["L1_conv_out_proj_w"].T
    d["conv_w"] = i["L1_conv_conv_w"].reshape(CP, 9)
    d["conv_b"] = i["L1_conv_conv_b"].reshape(CP, 1)
    xp = i["L1_conv_x_proj_w"].transpose(2, 0, 1)
    d["xdt_w"] = xp[:, :, 0:R]
    d["xb_w"] = np.tile(xp[:, :, R:R + NS], (1, 1, DB))
    d["xc_w"] = np.tile(xp[:, :, R + NS:R + 2 * NS], (1, 1, DB))
    d["dt_w"] = i["L1_conv_dt_projs_w"].transpose(2, 0, 1)
    d["dt_b"] = i["L1_conv_dt_projs_b"].T
    d["a_log"] = i["L1_conv_A_logs"].reshape(KD, NG, DB, NS).transpose(2, 3, 0, 1).reshape(P, KD * NG)
    d["d_skip"] = i["L1_conv_Ds"].reshape(KD, CP).T
    d["ln_g"] = i["L1_conv_out_norm_g"].reshape(CP, 1)
    d["ln_b"] = i["L1_conv_out_norm_b"].reshape(CP, 1)
    return {k: np.ascontiguousarray(v) for k, v in d.items()}


def kernel(**inputs):
    import concourse.bacc as bacc
    from concourse.bass_utils import run_bass_kernel_spmd as run

    arrays = layout({k: np.asarray(v) for k, v in inputs.items()})
    nc = bacc.Bacc("TRN2", target_bir_lowering=False, num_devices=1)
    d = {k: nc.dram_tensor(f"in_{k}", a.shape, mybir.dt.from_np(a.dtype), kind="ExternalInput").ap()
         for k, a in arrays.items()}
    out = nc.dram_tensor("out", (B, NC, CP, N), F32, kind="ExternalOutput").ap()
    build(nc, d, out)
    r = run(nc, [{f"in_{k}": a for k, a in arrays.items()}], core_ids=[0])
    return r.results[0]["out"].transpose(0, 3, 1, 2).reshape(B, H, W, C)
```

```python
from contextlib import ExitStack

import numpy as np

import concourse.bass as bass
from concourse import mybir

F32 = mybir.dt.float32
F32R = mybir.dt.float32r
BF16 = mybir.dt.bfloat16
ALU = mybir.AluOpType
ACT = mybir.ActivationFunctionType
AX = mybir.AxisListType

B, H, W, C = 8, 32, 32, 192
N = H * W
NH, HD = 12, 16
CP = 96
NC = C // CP
P = 128
NT = N // P
HF = 512
NHF = N // HF
NBUF = 3
TURNS = NH // NBUF
QR = 3 * HD
TWO = (2, 1)
THREE = (3, 2, 1)
BR = sum(THREE) * HD
VC = 48
MR, MB = 2, 3
GROUP = 6
A_LOG_MAX = 84.0
CONSTANTS = 40
KD, NS, R = 4, 16, 12
DB = P // NS
NG = CP // DB
WIN = 7
KROWS = 10
STORED = {"A": (16 * 6, 16 * 6), "C": (16 * 10, 16 * 6), "D": (16 * 4, 16 * 4)}
FIRST_STORED = {L: (q // 2, k // 2) for L, (q, k) in STORED.items()}
HEAD_IN = {"A": 16 * 2 * len(THREE), "C": 16 * (2 * len(THREE) + len(TWO)), "D": 16 * (2 * len(TWO) + 1)}
MAX_IN = {"A": 16 * MB, "C": 16 * MB, "D": 16 * MR}
BIG = -1.0e30
FR = P // W



def constants():
    c = {}
    c["ident"] = np.eye(P, dtype=np.float32)
    ch = np.arange(CP)
    c["group"] = ((ch[:, None] // GROUP == ch[None, :] // GROUP) / GROUP).astype(np.float32)
    c["mean"] = np.full((CP, CP), 1.0 / CP, np.float32)
    rot = np.zeros((CP, CP), np.float32)
    for j in range(CP):
        d = j % HD
        if d < HD // 2:
            rot[j + HD // 2, j] = -1.0
        else:
            rot[j - HD // 2, j] = 1.0
    c["rot"] = rot
    tok = np.arange(N)
    hot = np.concatenate([np.arange(H)[:, None] == tok[None, :] // W,
                          np.arange(W)[:, None] == tok[None, :] % W]).astype(np.float32)
    c["onehot"] = np.concatenate([hot, hot])
    start = np.clip(np.arange(H) - WIN // 2, 0, H - WIN)
    seen = (np.arange(H)[:, None] >= start[None, :]) & (np.arange(H)[:, None] < start[None, :] + WIN)
    far = np.where(seen, 0.0, BIG).astype(np.float32)
    c["window"] = np.concatenate([far[:, tok // W], far[:, tok % W]]).astype(np.float32)
    p = np.arange(P)
    spread = np.zeros((CP, NG, P), np.float32)
    for g in range(NG):
        spread[DB * g + p // NS, g, p] = 1.0
    c["spread"] = spread
    c["gather"] = np.ascontiguousarray(spread.transpose(2, 1, 0))
    lo = np.zeros((QR, 1), np.float32)
    lo[2 * HD:3 * HD] = -1.0
    c["lorows"] = lo
    c["spread"] = np.concatenate([c["spread"], c["spread"][:, 0:2]], axis=1)
    c["gather"] = np.concatenate([c["gather"], c["gather"][:, 0:2]], axis=1)
    return c



ATTN = ("A", "C", "D")
BIASED = ("A", "C")


class Space:
    pass


class NormSignals:
    def __init__(self, sem, L):
        self.stats = sem(f"{L}_stats")
        self.stat_sums = sem(f"{L}_stat_sums")
        self.var = sem(f"{L}_var")
        self.rstd = sem(f"{L}_rstd")
        self.xn = sem(f"{L}_xn")


class AttentionSignals(NormSignals):
    def __init__(self, sem, L):
        NormSignals.__init__(self, sem, L)
        self.qk_ps = sem(f"{L}_qk_ps")
        self.raw = sem(f"{L}_raw")
        if L == "A":
            self.rot_ps = sem(f"{L}_rot_ps")
        self.split = sem(f"{L}_split")
        self.v_ps = sem(f"{L}_v_ps")
        self.v_used = sem(f"{L}_v_used")
        self.s_ps = sem(f"{L}_s_ps")
        self.mx_used = sem(f"{L}_mx_used")
        self.mx = sem(f"{L}_mx")
        self.mt = sem(f"{L}_mt")
        self.nm = sem(f"{L}_nm")
        self.nm_in = sem(f"{L}_nm_in")
        self.vh = sem(f"{L}_vh")
        self.st_ps = sem(f"{L}_st_ps")
        self.pt = sem(f"{L}_pt")
        self.pt_used = sem(f"{L}_pt_used")
        self.o_used = sem(f"{L}_o_used")
        self.sums = sem(f"{L}_sums")
        self.o = sem(f"{L}_o")
        self.o_out = [sem(f"{L}_o_out{i}") for i in range(NBUF)]
        self.ocm_in = sem(f"{L}_ocm_in")
        self.proj_ps = sem(f"{L}_proj_ps")
        self.x_done = sem(f"{L}_x_done")
        if L == "C":
            self.rq_ps = sem(f"{L}_rq_ps")
            self.rq_hi = sem(f"{L}_rq_hi")
            self.rq = sem(f"{L}_rq")
        self.stored = [sem(f"{L}_stored{i}") for i in range(2)]
        self.heads = [sem(f"{L}_heads{i}") for i in range(NBUF)]


class ScanSignals(NormSignals):
    def __init__(self, sem, L):
        NormSignals.__init__(self, sem, L)
        self.xz_ps = sem(f"{L}_xz_ps")
        self.xh = sem(f"{L}_xh")
        self.z = sem(f"{L}_z")
        self.u_conv = sem(f"{L}_u_conv")
        self.u_exp = sem(f"{L}_u_exp")
        self.u = sem(f"{L}_u")
        self.dtr_ps = sem(f"{L}_dtr_ps")
        self.dtr = sem(f"{L}_dtr")
        self.dtp_ps = sem(f"{L}_dtp_ps")
        self.v = sem(f"{L}_v")
        self.e = sem(f"{L}_e")
        self.dt_split = sem(f"{L}_dt_split")
        self.brep_ps = sem(f"{L}_brep_ps")
        self.brep = sem(f"{L}_brep")
        self.crep_ps = sem(f"{L}_crep_ps")
        self.crep = sem(f"{L}_crep")
        self.sel = sem(f"{L}_sel")
        self.dtb_ps = sem(f"{L}_dtb_ps")
        self.da = sem(f"{L}_da")
        self.dub_ps = sem(f"{L}_dub_ps")
        self.bt = sem(f"{L}_bt")
        self.h = sem(f"{L}_h")
        self.hc = sem(f"{L}_hc")
        self.y_used = sem(f"{L}_y_used")
        self.ysb = sem(f"{L}_ysb")
        self.mean_ps = sem(f"{L}_mean_ps")
        self.sq = sem(f"{L}_sq")
        self.var_ps = sem(f"{L}_var_ps")
        self.rln = sem(f"{L}_rln")
        self.yz = sem(f"{L}_yz")
        self.out_ps = sem(f"{L}_out_ps")
        self.x_done = sem(f"{L}_x_done")


def allocate(nc, ctx):
    m = Space()

    def sb(stack, name, shape, dt=F32):
        return stack.enter_context(nc.sbuf_tensor(name, shape, dt))

    def ps(name, shape):
        return ctx.enter_context(nc.psum_tensor(name, shape, F32))

    m.s1 = ps("s1", [P, 2, HF])
    m.s2 = ps("s2", [P, 2, N])
    m.px = ps("px", [P, 2, HF])

    m.x = sb(ctx, "x", [CP, NC, N])
    m.xn = sb(ctx, "xn", [CP, NC, N])
    m.gn = sb(ctx, "gn", [CP, NC, 2, 6])
    m.mv = sb(ctx, "mv", [CP, NC, 2])
    m.gs = sb(ctx, "gs", [CP, NC, 2])
    m.gt = sb(ctx, "gt", [CP, NC])
    m.gv = sb(ctx, "gv", [CP, NC])
    m.gl = sb(ctx, "gl", [CP, NC])
    m.gr = sb(ctx, "gr", [CP, NC])
    m.eps = sb(ctx, "eps", [CP, 1])
    m.ident = sb(ctx, "ident", [P, P])
    m.group = sb(ctx, "group", [CP, CP])
    m.mean = sb(ctx, "mean", [CP, CP])
    m.rot = sb(ctx, "rot", [CP, CP])
    m.qs = [sb(ctx, f"qs{i}", [P, N], F32R) for i in range(NBUF)]
    m.ks = [sb(ctx, f"ks{i}", [P, N], F32R) for i in range(NBUF)]
    m.qb = [sb(ctx, f"qb{i}", [BR + MB, N], BF16) for i in range(NBUF)]
    m.kb = [sb(ctx, f"kb{i}", [BR + MB, N], BF16) for i in range(NBUF)]
    m.den = sb(ctx, "den", [P, N // 4])
    m.vh = [sb(ctx, f"vh{i}", [P, NT, VC]) for i in range(NBUF)]
    m.hot = sb(ctx, "hot", [P, N], F32R)
    m.v = sb(ctx, "v", [P, NT, NH, HD])
    m.w = {}
    for L in ATTN:
        m.w[L] = Space()
        m.w[L].qkv = sb(ctx, f"qkv_w{L}", [CP, NC, 3 * C])
        m.w[L].proj = sb(ctx, f"proj_w{L}", [CP, NC, C])
        if L in BIASED:
            m.w[L].qkb = sb(ctx, f"qk_b{L}", [CP, 4])
            m.w[L].vb = sb(ctx, f"v_b{L}", [P, 2, NH, HD])
            m.w[L].pb = sb(ctx, f"proj_b{L}", [CP, NC])
    m.relh = sb(ctx, "relh", [QR, H, H], F32R)
    m.relw = sb(ctx, "relw", [QR, W, W], F32R)
    m.inw = sb(ctx, "inw", [CP, NC, C])
    m.outw = sb(ctx, "outw", [CP, C])
    m.convw = sb(ctx, "convw", [CP, 9])
    m.convb = sb(ctx, "convb", [CP, 1])
    m.xdtw = sb(ctx, "xdtw", [CP, KD, R])
    m.xbw = sb(ctx, "xbw", [CP, KD, P])
    m.xcw = sb(ctx, "xcw", [CP, KD, P])
    m.dtw = sb(ctx, "dtw", [R, KD, CP])
    m.dtb = sb(ctx, "dtb", [CP, KD])
    m.arow = sb(ctx, "arow", [P, KD * NG])
    m.dskip = sb(ctx, "dskip", [CP, KD])
    m.diag = sb(ctx, "diag", [CP, CP])
    m.spread_t = sb(ctx, "spread_t", [CP, NG + 2, P], F32R)
    m.gather_t = sb(ctx, "gather_t", [P, NG + 2, CP])
    m.spread = sb(ctx, "spread", [CP, 4, P], F32R)
    m.gather = sb(ctx, "gather", [P, 4, CP])
    m.lorows = sb(ctx, "lorows", [QR, 1])
    m.lng = sb(ctx, "lng", [CP, 1])
    m.lnb = sb(ctx, "lnb", [CP, 1])

    with ExitStack() as stage:
        m.hot_in = sb(stage, "hot_in", [P, N])
        m.window_in = sb(stage, "window_in", [P, N])
        m.spread_in = sb(stage, "spread_in", [CP, NG + 2, P])
        m.rel_in = [sb(stage, f"rel_in{i}", [QR, H, H]) for i in range(2)]
        m.zeros = sb(stage, "zeros", [MR, N])
    with ExitStack() as split:
        m.cos = sb(split, "cos", [CP, N])
        m.sin = sb(split, "sin", [CP, N])
        m.raw = [sb(split, f"raw{i}", [CP, N]) for i in range(2)]
        m.ra = sb(split, "ra", [CP, N])
        m.rb = sb(split, "rb", [CP, N])
        m.hi = [sb(split, f"hi{i}", [CP, N], F32R) for i in range(2)]
        m.lo = [sb(split, f"lo{i}", [CP, N], F32R) for i in range(2)]
        m.part = [sb(split, f"part{i}", [CP, 3, N], BF16) for i in range(2)]
    with ExitStack() as heads:
        m.pt = [sb(heads, f"pt{i}", [P, N]) for i in range(4)]
        m.rq = [sb(heads, f"rq{i}", [P, N], F32R) for i in range(NBUF)]
        m.sums = sb(heads, "sums", [HD, N])
        m.rc = sb(heads, "rc", [P, N // 4])
        m.o = [sb(heads, f"o{i}", [HD, N]) for i in range(NBUF)]
        m.ocm = sb(heads, "ocm", [CP, NC, N])
        m.mxp = sb(heads, "mxp", [P, NT, NHF])
        m.mx = sb(heads, "mx", [P, NT])
        m.nm = sb(heads, "nm", [NT, MR, P], F32R)
        m.nb = sb(heads, "nb", [NT, MB, P], BF16)
        m.nr = sb(heads, "nr", [NT, P])
    with ExitStack() as scan:
        m.pad = sb(scan, "pad", [CP, H + 2, W + 2])
        m.zs = sb(scan, "zs", [CP, N])
        m.u = sb(scan, "u", [CP, 2, N])
        m.t0 = sb(scan, "t0", [CP, N])
        m.t1 = sb(scan, "t1", [CP, N])
        m.dtr = m.xn[0:R, 0, :]
        m.dt = m.xn[:, 1, :]
        m.du = sb(scan, "du", [CP, N])
        m.dth = sb(scan, "dth", [CP, 2, N], F32R)
        m.duh = sb(scan, "duh", [CP, 2, N], F32R)
        m.brep = sb(scan, "brep", [P, N])
        m.crep = sb(scan, "crep", [P, N])
        m.da = [sb(scan, f"da{i}", [P, N]) for i in range(2)]
        m.bt = [sb(scan, f"bt{i}", [P, N]) for i in range(2)]
        m.hs = [sb(scan, f"hs{i}", [P, N]) for i in range(2)]
        m.z = m.hs[0][0:CP]
        m.hc = [sb(scan, f"hc{i}", [P, N]) for i in range(2)]

    m.qd = nc.dram_tensor("q_split", (2, C, N), F32, kind="Internal").ap()
    m.kd = nc.dram_tensor("k_split", (2, C, N), F32, kind="Internal").ap()

    m.qp = nc.dram_tensor("q_parts", (3, C, N), BF16, kind="Internal").ap()
    m.kp = nc.dram_tensor("k_parts", (3, C, N), BF16, kind="Internal").ap()
    m.od = nc.dram_tensor("head_outputs", (C, N), F32, kind="Internal").ap()
    m.zero = nc.dram_tensor("zero_rows", (MR, N), F32, kind="Internal").ap()

    def sem(name):
        return ctx.enter_context(nc.semaphore(name))

    m.const_in = sem("const_in")
    m.const_ready = sem("const_ready")
    m.a_log = sem("a_log")
    m.zero_in = sem("zero_in")
    m.a_exp = sem("a_exp")
    m.x_in = sem("x_in")
    m.rope_in = sem("rope_in")
    m.settled = sem("settled")
    m.out_done = sem("out_done")
    m.s = {L: AttentionSignals(sem, L) for L in ATTN}
    m.s["B"] = ScanSignals(sem, "B")
    return m



def norm_vector(nc, dve, m, L, b):
    s = m.s[L]
    for c in range(NC):
        for f in range(NHF):
            nc.vector.bn_stats(m.gn[:, c, f, :], m.x[:, c, f * HF:(f + 1) * HF])
    nc.vector.drain()
    for c in range(NC):
        nc.vector.bn_aggr(m.mv[:, c, :], m.gn[:, c, :, :])
    nc.vector.drain()
    nc.vector.tensor_tensor(m.gt[:], m.mv[:, :, 0], m.mv[:, :, 0], ALU.mult)
    nc.vector.drain()
    nc.vector.tensor_tensor(m.mv[:, :, 1], m.mv[:, :, 1], m.gt[:], ALU.add).then_inc(s.stats, 1)
    dve.wait_ge(s.stat_sums, b + 1)
    nc.vector.tensor_copy(m.gs[:], m.px[0:CP, 1, 0:2 * NC].rearrange("p (c s) -> p c s", c=NC))
    nc.vector.drain()
    nc.vector.tensor_tensor(m.gt[:], m.gs[:, :, 0], m.gs[:, :, 0], ALU.mult)
    nc.vector.drain()
    nc.vector.tensor_tensor(m.gv[:], m.gs[:, :, 1], m.gt[:], ALU.subtract).then_inc(s.var, 1)
    dve.wait_ge(s.rstd, b + 1)
    for c in range(NC):
        nc.vector.tensor_scalar(m.xn[:, c, :], m.x[:, c, :], m.gs[:, c, 0:1], m.gr[:, c:c + 1],
                                ALU.subtract, ALU.mult).then_inc(s.xn, 1)


def norm_scalar(nc, act, m, L, b):
    s = m.s[L]
    act.wait_ge(s.var, b + 1)
    nc.scalar.activation(m.gl[:], m.gv[:], ACT.Ln, bias=m.eps[:, 0:1])
    nc.scalar.drain()
    nc.scalar.activation(m.gr[:], m.gl[:], ACT.Exp, scale=-0.5).then_inc(s.rstd, 1)


def norm_tensor(nc, pe, m, L, b):
    s = m.s[L]
    pe.wait_ge(s.stats, b + 1)
    nc.tensor.matmul(m.px[0:CP, 1, 0:2 * NC], m.group[:], m.mv[:].rearrange("p c s -> p (c s)"),
                     start=True, stop=True).then_inc(s.stat_sums, 1)



def spans(L):
    if L == "D":
        keys = [(W * min(max(FR * t - WIN // 2, 0), H - KROWS), W * KROWS) for t in range(NT)]
        queries = [(P * min(max(t - 1, 0), NT - 3), 3 * P) for t in range(NT)]
    else:
        keys = queries = [(0, N)] * NT
    return keys, queries


def seen_by(L, f):
    _, queries = spans(L)
    return min(t for t, (q0, n) in enumerate(queries) if q0 < (f + 1) * HF and q0 + n > f * HF)


def pieces(L):
    keys, _ = spans(L)
    return [(t, k0 + o, min(HF, n)) for t, (k0, n) in enumerate(keys) for o in range(0, n, HF)]


def quarter(i):
    return slice(i * N // 4, (i + 1) * N // 4)


def by_image(m, axis):
    rows = m.s1[0:H, :, :].rearrange("p a n -> p (a n)")
    return rows.rearrange("p (c r) -> p r c", r=H) if axis else rows.rearrange("p (r c) -> p r c", r=H)


JOBS = [(0, 0), (1, 0), (0, 1), (1, 1)]


def heads_loop(eng, body):
    with eng.Fori(0, TURNS - 1) as j:
        for u in range(NBUF):
            body(j, u, 2)
    for u in range(NBUF):
        body(TURNS - 1, u, NBUF - 1 - u)


def settle(eng, m):
    eng.sem_inc(m.settled, 1)


def following(j, u):
    return (j + 1, 0) if u == NBUF - 1 else (j, u + 1)


def attn_tensor(nc, pe, m, L, b):
    s, w = m.s[L], m.w[L]
    keys, queries = spans(L)
    norm_tensor(nc, pe, m, L, b)
    pe.wait_ge(s.xn, NC * b + NC)
    for i, (which, c) in enumerate(JOBS):
        if i >= 2:
            pe.wait_ge(s.raw, 4 * b + i - 1)
        for f in range(NHF):
            for kc in range(NC):
                last = nc.tensor.matmul(
                    m.s2[0:CP, i % 2, f * HF:(f + 1) * HF],
                    w.qkv[:, kc, which * C + c * CP:which * C + (c + 1) * CP],
                    m.xn[:, kc, f * HF:(f + 1) * HF], start=kc == 0, stop=kc == NC - 1)
        last.then_inc(s.qk_ps, 1)
        if L == "A":
            pe.wait_ge(s.raw, 4 * b + i + 1)
            if i >= 1:
                pe.wait_ge(s.split, 4 * b + i)
            for f in range(NHF):
                last = nc.tensor.matmul(m.s1[0:CP, f, :], m.rot[:], m.raw[i % 2][:, f * HF:(f + 1) * HF],
                                        start=True, stop=True)
            last.then_inc(s.rot_ps, 1)
    for i in range(NT // 2):
        if i < 2:
            pe.wait_ge(s.raw, 4 * b + i + 3)
        else:
            pe.wait_ge(s.v_used, 4 * b + i - 1)
        for a in range(2):
            t = 2 * i + a
            for kc in range(NC):
                last = nc.tensor.matmul(m.s2[:, i % 2, a * C:(a + 1) * C], m.xn[:, kc, t * P:(t + 1) * P],
                                        w.qkv[:, kc, 2 * C:3 * C], start=kc == 0, stop=kc == NC - 1)
        last.then_inc(s.v_ps, 1)
    pe.wait_ge(s.v_used, 4 * b + 4)

    todo = pieces(L)
    per = len(todo)

    def last_maxima_read(h):
        if not (isinstance(h, int) and h == 0):
            pe.wait_ge(s.nm, NH * b + h)

    def relative(h, u, axis):
        if axis == 0:
            last_maxima_read(h)
        else:
            pe.wait_ge(s.rq, 2 * (NH * b + h) + 1)
        settle(pe, m)
        table = (m.relh, m.relw)[axis]
        for r in range(H):
            q = m.qs[u][0:QR, r:N:W] if axis else m.qs[u][0:QR, r * W:(r + 1) * W]
            last = nc.tensor.matmul(m.s1[0:H, r * W // HF, (r * W) % HF:(r * W) % HF + W], table[:, r, :], q,
                                    start=True, stop=True)
        last.then_inc(s.rq_ps, 1)

    def first(j, u, i):
        h = j * NBUF + u
        t, k0, n = todo[i]
        out = m.s1[:, i % 2, 0:n]
        q = slice(t * P, (t + 1) * P)
        if L == "C" and i == 0:
            pe.wait_ge(s.rq, 2 * (NH * b + h) + 2)
        elif i == 0:
            last_maxima_read(h)
        if i >= 2:
            pe.wait_ge(s.mx_used, NH * per * b + per * h + i)
        if L == "D":
            last = nc.tensor.matmul(out, m.qs[u][:, q], m.ks[u][:, k0:k0 + n], start=True, stop=True)
        else:
            last = nc.tensor.matmul(out, m.qb[u][0:BR, q], m.kb[u][0:BR, k0:k0 + n], start=True, stop=L == "A")
        if L == "C":
            last = nc.tensor.matmul(out, m.rq[u][:, q], m.hot[:, k0:k0 + n], start=False, stop=True)
        last.then_inc(s.s_ps, 1)

    def begin(j, u):
        h = j * NBUF + u
        pe.wait_ge(s.heads[u], HEAD_IN[L] * (TURNS * b + j + 1))
        if L == "C":
            relative(h, u, 0)

    def maxima(h):
        pe.wait_ge(s.mx, NH * b + h + 1)
        nc.tensor.transpose(m.s1[0:NT, 0, 0:P], m.mx[:], m.ident[:]).then_inc(s.mt, 1)

    def second(h, u, t):
        q0, n = queries[t]
        k = slice(t * P, (t + 1) * P)
        if t == 0:
            pe.wait_ge(s.nm_in, MAX_IN[L] * (NH * b + h + 1))
        pe.wait_ge(s.pt, NH * NT * b + NT * h + t + 1)
        for f0 in range(0, n, HF):
            nf = min(HF, n - f0)
            out = m.s2[:, t % 2, f0:f0 + nf]
            kk, qq = (m.ks[u], m.qs[u]) if L == "D" else (m.kb[u], m.qb[u])
            last = nc.tensor.matmul(out, kk[:, k], qq[:, q0 + f0:q0 + f0 + nf], start=True, stop=L != "C")
            if L == "C":
                last = nc.tensor.matmul(out, m.hot[:, k], m.rq[u][:, q0 + f0:q0 + f0 + nf],
                                        start=False, stop=True)
        last.then_inc(s.st_ps, 1)

    def values(h, u, t):
        q0, n = queries[t]
        pe.wait_ge(s.pt, NH * NT * b + NT * h + t + 3)
        if t == 0:
            pe.wait_ge(s.o_used, NH * b + h + 1)
            pe.wait_ge(s.sums, NH * b + h + 1)
            pe.wait_ge(s.vh, NH * b + h + 1)
        for f in range(NHF):
            lo, hi = max(q0, f * HF), min(q0 + n, (f + 1) * HF)
            if lo < hi:
                last = nc.tensor.matmul(m.px[0:VC, f, lo - f * HF:hi - f * HF], m.vh[u][:, t, :],
                                        m.pt[t % 4][:, lo - q0:hi - q0], start=t == seen_by(L, f),
                                        stop=t == NT - 1, skip_group_check=True)
        last.then_inc(s.pt_used, 1)

    def body(j, u, ahead):
        h = j * NBUF + u
        nj, nu = following(*following(j, u))
        t0 = 3 if L == "C" else 1
        for t in range(NT):
            second(h, u, t)
            if ahead >= 2 and L == "C" and t == 2:
                relative(nj * NBUF + nu, nu, 1)
            mine = range(max(t - t0, 0) * per // (NT - t0), max(t - t0 + 1, 0) * per // (NT - t0))
            early = 2 if t > 1 else 0
            if ahead >= 2:
                for i in mine[:early]:
                    first(nj, nu, i)
            if t >= 1:
                values(h, u, t - 1)
            if ahead >= 2:
                if t == 1:
                    begin(nj, nu)
                for i in mine[early:]:
                    first(nj, nu, i)
        values(h, u, NT - 1)
        if ahead >= 2:
            maxima(h + 2)

    for u in range(2):
        begin(0, u)
        if L == "C":
            relative(u, u, 1)
        for i in range(per):
            first(0, u, i)
        maxima(u)
    heads_loop(pe, body)
    pe.wait_ge(s.pt, NH * NT * (b + 1) + 2)
    pe.wait_ge(s.ocm_in, 16 * (b + 1))
    for c in range(NC):
        for f in range(NHF):
            for kc in range(NC):
                out = m.s1[0:CP, f, :] if c == 0 else m.s2[0:CP, 0, f * HF:(f + 1) * HF]
                last = nc.tensor.matmul(out, w.proj[:, kc, c * CP:(c + 1) * CP],
                                        m.ocm[:, kc, f * HF:(f + 1) * HF], start=kc == 0, stop=kc == NC - 1)
        last.then_inc(s.proj_ps, 1)


def attn_scalar(nc, act, m, L, b):
    s, w = m.s[L], m.w[L]
    _, queries = spans(L)
    norm_scalar(nc, act, m, L, b)
    for i, (which, c) in enumerate(JOBS):
        act.wait_ge(s.qk_ps, 4 * b + i + 1)
        if i >= 2:
            act.wait_ge(s.split, 4 * b + i - 1)
        scale = HD ** -0.5 if L == "C" and which == 1 else 1.0
        if L in BIASED:
            nc.scalar.activation(m.raw[i % 2][:], m.s2[0:CP, i % 2, :], ACT.Identity,
                                 bias=w.qkb[:, 2 * which + c:2 * which + c + 1], scale=scale).then_inc(s.raw, 1)
        else:
            nc.scalar.activation(m.raw[i % 2][:], m.s2[0:CP, i % 2, :], ACT.Copy).then_inc(s.raw, 1)

    def relative(h, u, axis):
        act.wait_ge(s.rq_ps, 2 * (NH * b + h) + axis + 1)
        nc.scalar.activation(m.rq[u][axis * H:(axis + 1) * H, :].rearrange("p (r c) -> p r c", r=H),
                             by_image(m, axis), ACT.Copy).then_inc(s.rq_hi, 1)

    def body(j, u, ahead):
        h = j * NBUF + u
        nj, nu = following(*following(j, u))
        for t in range(NT):
            if ahead >= 2 and L == "C" and t in (2, 3):
                relative(nj * NBUF + nu, nu, t - 2)
            n = queries[t][1]
            act.wait_ge(s.st_ps, NH * NT * b + NT * h + t + 1)
            act.wait_ge(s.pt_used, NH * NT * b + NT * h + t + 1)
            nc.scalar.activation(m.pt[t % 4][:, 0:n], m.s2[:, t % 2, 0:n], ACT.Exp,
                                 scale=1.0 if L == "C" else HD ** -0.5).then_inc(s.pt, 1)
        act.wait_ge(s.pt_used, NH * NT * b + NT * h + NT + 4)
        act.wait_ge(s.o, NH * b + h + 1)
        nc.scalar.activation(m.sums[:], m.px[0:HD, :, :].rearrange("p a n -> p (a n)"), ACT.Copy) \
            .then_inc(s.sums, 1)

    if L == "C":
        for i in range(2):
            act.wait_ge(s.stored[i], STORED[L][i] * (b + 1))
        for u in range(2):
            for axis in range(2):
                relative(u, u, axis)
    heads_loop(act, body)


def attn_vector(nc, dve, m, L, b):
    s, w = m.s[L], m.w[L]
    norm_vector(nc, dve, m, L, b)
    if L == "A":
        dve.wait_ge(m.rope_in, 32 * b + 32)
    for i, (which, c) in enumerate(JOBS):
        dve.wait_ge(s.raw, 4 * b + i + 1)
        src = m.raw[i % 2]
        if L == "A":
            nc.vector.tensor_tensor(m.ra[:], src[:], m.cos[:], ALU.mult)
            dve.wait_ge(s.rot_ps, 4 * b + i + 1)
            nc.vector.tensor_tensor(m.rb[:], m.s1[0:CP, :, :].rearrange("p a n -> p (a n)"), m.sin[:], ALU.mult)
            nc.vector.drain()
            nc.vector.tensor_tensor(src[:], m.ra[:], m.rb[:], ALU.add)
            nc.vector.drain()
        if i >= 2:
            dve.wait_ge(s.stored[i % 2], STORED[L][i % 2] * b + FIRST_STORED[L][i % 2])
        if L != "A" and not (L == "C" and which == 1):
            nc.vector.tensor_copy(m.hi[i % 2][:], src[:])
            nc.vector.drain()
            last = nc.vector.tensor_tensor(m.lo[i % 2][:], src[:], m.hi[i % 2][:].bitcast(F32), ALU.subtract)
        if L != "D":
            part = m.part[i % 2]
            nc.vector.tensor_copy(part[:, 0, :], src[:])
            nc.vector.drain()
            nc.vector.tensor_tensor(src[:], src[:], part[:, 0, :], ALU.subtract)
            nc.vector.drain()
            nc.vector.tensor_copy(part[:, 1, :], src[:])
            nc.vector.drain()
            last = nc.vector.tensor_tensor(part[:, 2, :], src[:], part[:, 1, :], ALU.subtract)
        last.then_inc(s.split, 1)
    for i in range(NT // 2):
        dve.wait_ge(s.v_ps, 4 * b + i + 1)
        for a in range(2):
            dst = m.v[:, 2 * i + a, :, :]
            psum = m.s2[:, i % 2, a * C:(a + 1) * C].rearrange("p (h d) -> p h d", h=NH)
            if L in BIASED:
                last = nc.vector.tensor_tensor(dst, psum, w.vb[:, a, :, :], ALU.add)
            else:
                last = nc.vector.tensor_copy(dst, psum)
        last.then_inc(s.v_used, 1)

    todo = pieces(L)
    per = len(todo)
    halves = per // NT

    def relative(h, u):
        for axis in range(2):
            dve.wait_ge(s.rq_hi, 2 * (NH * b + h) + axis + 1)
            hi = m.rq[u][axis * H:(axis + 1) * H, :].bitcast(F32).rearrange("p (r c) -> p r c", r=H)
            lo = m.rq[u][(axis + 2) * H:(axis + 3) * H, :].rearrange("p (r c) -> p r c", r=H)
            nc.vector.tensor_tensor(lo, by_image(m, axis), hi, ALU.subtract).then_inc(s.rq, 1)

    def first(h, u):
        for i, (t, _, n) in enumerate(todo):
            dve.wait_ge(s.s_ps, NH * per * b + per * h + i + 1)
            out = m.mxp[:, t, i % 2:i % 2 + 1] if halves == 2 else m.mx[:, t:t + 1]
            last = nc.vector.tensor_reduce(out, m.s1[:, i % 2, 0:n], AX.X, ALU.max).then_inc(s.mx_used, 1)
        if halves == 2:
            nc.vector.drain()
            nc.vector.tensor_reduce(m.mx[:], m.mxp[:], AX.X, ALU.max)
        nc.vector.drain().then_inc(s.mx, 1)

    def negated(h):
        dve.wait_ge(s.mt, NH * b + h + 1)
        if not (isinstance(h, int) and h == 0):
            dve.wait_ge(s.nm_in, MAX_IN[L] * (NH * b + h))
        mt = m.s1[0:NT, 0, 0:P]
        if L == "D":
            nc.vector.tensor_scalar(m.nm[:, 0, :], mt, -1.0, None, ALU.mult)
            nc.vector.drain()
            nc.vector.scalar_tensor_tensor(m.nm[:, 1, :], mt, -1.0, m.nm[:, 0, :].bitcast(F32),
                                           ALU.mult, ALU.subtract).then_inc(s.nm, 1)
        else:
            nc.vector.tensor_scalar(m.nb[:, 0, :], mt, -1.0, None, ALU.mult)
            nc.vector.drain()
            nc.vector.scalar_tensor_tensor(m.nr[:], mt, -1.0, m.nb[:, 0, :], ALU.mult, ALU.subtract)
            nc.vector.drain()
            nc.vector.tensor_copy(m.nb[:, 1, :], m.nr[:])
            nc.vector.drain()
            nc.vector.tensor_tensor(m.nb[:, 2, :], m.nr[:], m.nb[:, 1, :], ALU.subtract).then_inc(s.nm, 1)

    def denominators(h):
        nc.vector.drain()
        dve.wait_ge(s.pt_used, NH * NT * b + NT * h + NT + 4)
        px = m.px[:].rearrange("p a n -> p (a n)")
        for i in range(4):
            last = nc.vector.tensor_copy(m.den[32 * i:32 * i + HD, :], px[32:32 + HD, quarter(i)])
        last.then_inc(s.o_used, 1)

    def divide(j, u):
        h = j * NBUF + u
        nc.vector.drain()
        nc.vector.reciprocal(m.rc[:], m.den[:])
        nc.vector.drain()
        dve.wait_ge(s.sums, NH * b + h + 2)
        dve.wait_ge(s.o_out[u], 16 * (TURNS * b + j) + 16)
        for i in range(4):
            last = nc.vector.tensor_tensor(m.o[u][:, quarter(i)], m.sums[:, quarter(i)],
                                           m.rc[32 * i:32 * i + HD, :], ALU.mult)
        last.then_inc(s.o, 1)

    def body(j, u, ahead):
        h = j * NBUF + u
        if ahead >= 2:
            nj, nu = following(*following(j, u))
            if L == "C":
                relative(nj * NBUF + nu, nu)
            first(nj * NBUF + nu, nu)
        denominators(h)
        if ahead >= 2:
            negated(h + 2)
        divide(j, u)

    for u in range(2):
        if L == "C":
            relative(u, u)
        first(u, u)
        negated(u)
    heads_loop(dve, body)
    for c in range(NC):
        dve.wait_ge(s.proj_ps, NC * b + c + 1)
        psum = m.s1[0:CP, :, :].rearrange("p a n -> p (a n)") if c == 0 else m.s2[0:CP, 0, :]
        if L in BIASED:
            nc.vector.scalar_tensor_tensor(m.x[:, c, :], psum, w.pb[:, c:c + 1], m.x[:, c, :],
                                           ALU.add, ALU.add).then_inc(s.x_done, 1)
        else:
            nc.vector.tensor_tensor(m.x[:, c, :], psum, m.x[:, c, :], ALU.add).then_inc(s.x_done, 1)
    nc.vector.drain()


def attn_sync(nc, sp, m, L, b):
    s = m.s[L]
    def split(i, which, c):
        sp.wait_ge(s.split, 4 * b + i + 1)
        rows = slice(c * CP, (c + 1) * CP)
        if L == "D" or (L == "C" and which == 0):
            for part, src in enumerate((m.hi, m.lo)):
                sp.dma_start((m.qd, m.kd)[which][part, rows, :], src[i % 2][:].bitcast(F32)) \
                    .then_inc(s.stored[i % 2], 16)
        if L != "D":
            for part in range(3):
                sp.dma_start((m.qp, m.kp)[which][part, rows, :], m.part[i % 2][:, part, :]) \
                    .then_inc(s.stored[i % 2], 16)

    def load(j, u):
        row = (j * NBUF + u) * HD
        if L == "D":
            todo = [(m.qs, m.qd, TWO, "q"), (m.ks, m.kd, TWO, "k")]
        else:
            todo = [(m.qb, m.qp, THREE, "q"), (m.kb, m.kp, THREE, "k")]
        if L == "C":
            todo.append((m.qs, m.qd, TWO, "q"))
        for dst, src, counts, side in todo:
            r = 0
            for part, n in enumerate(counts):
                to = dst[u][r * HD:(r + n) * HD, :]
                if side == "q":
                    parts = src[0:n, bass.ds(row, HD), :]
                else:
                    parts = src[part:part + 1, bass.ds(row, HD), :].broadcast_to([n, HD, N])
                if src in (m.qd, m.kd):
                    to = to.bitcast(F32)
                sp.dma_start(to, parts).then_inc(s.heads[u], 16)
                r += n
        if L == "D":
            sp.dma_start(m.qs[u][QR:QR + MR, :].bitcast(F32), m.zero).then_inc(s.heads[u], 16)

    def maxima(h, u):
        sp.wait_ge(s.nm, NH * b + h + 1)
        for r in range(MR if L == "D" else MB):
            if L == "D":
                dst, src = m.qs[u][QR + r:QR + r + 1, :].bitcast(F32), m.nm[:, r, :].bitcast(F32)
            else:
                dst, src = m.qb[u][BR + r:BR + r + 1, :], m.nb[:, r, :]
            sp.dma_start(dst.rearrange("r (t n) -> r t n", t=NT), src).then_inc(s.nm_in, 16)

    def store(j, u):
        h = j * NBUF + u
        sp.wait_ge(s.o, NH * b + h + 2)
        settle(sp, m)
        sp.dma_start(m.od[bass.ds(h * HD, HD), :], m.o[u][:]).then_inc(s.o_out[u], 16)

    def body(j, u, ahead):
        h = j * NBUF + u
        if not isinstance(j, int):
            sp.wait_ge(s.st_ps, NH * NT * b + NT * h + NT)
            settle(sp, m)
            load(j + 1, u)
        if ahead >= 2:
            maxima(h + 2, (u + 2) % NBUF)
        store(j, u)

    for i in range(2):
        split(i, *JOBS[i])
    for i in range(2):
        sp.wait_ge(s.stored[i], STORED[L][i] * b + FIRST_STORED[L][i])
    load(0, 0)
    for i in range(2, 4):
        split(i, *JOBS[i])
    for u in range(1, NBUF):
        load(0, u)
    for i in range(2):
        sp.wait_ge(s.stored[i], STORED[L][i] * (b + 1))
    for u in range(2):
        maxima(u, u)
    heads_loop(sp, body)
    for u in range(NBUF):
        sp.wait_ge(s.o_out[u], 16 * TURNS * (b + 1) + 16)
    sp.dma_start(m.ocm[:], m.od.rearrange("(c p) n -> p c n", c=NC)).then_inc(s.ocm_in, 16)



TILES = KD * NG


def scan_order(ap, k):
    return ap[:, ::-1] if k >= 2 else ap


def scan_tensor(nc, pe, m, b):
    s = m.s["B"]
    norm_tensor(nc, pe, m, "B", b)
    pe.wait_ge(s.xn, NC * b + NC)
    for o in range(2):
        for f in range(NHF):
            for kc in range(NC):
                last = nc.tensor.matmul(m.s2[0:CP, o, f * HF:(f + 1) * HF], m.inw[:, kc, o * CP:(o + 1) * CP],
                                        m.xn[:, kc, f * HF:(f + 1) * HF], start=kc == 0, stop=kc == NC - 1)
        last.then_inc(s.xz_ps, 1)
    pe.wait_ge(s.u, b + 1)
    for f in range(NHF):
        nc.tensor.matmul(m.px[0:CP, f, :], m.diag[:], m.u[:, 0, f * HF:(f + 1) * HF],
                         start=True, stop=False, skip_group_check=True)

    def tile(k, g, v):
        i = TILES * b + NG * k + g
        pe.wait_ge(s.sel, i + 1)
        pe.wait_ge(s.da, i + 1)
        for f in range(NHF):
            for part in range(2):
                last = nc.tensor.matmul(m.s1[:, f, :], m.spread[:, v, :], m.dth[:, part, f * HF:(f + 1) * HF],
                                        start=part == 0, stop=part == 1)
        last.then_inc(s.dtb_ps, 1)
        if isinstance(g, int) and g == 0:
            pe.wait_ge(s.dt_split, 2 * (KD * b + k) + 2)
        pe.wait_ge(s.bt, i + 1)
        for f in range(NHF):
            for part in range(2):
                last = nc.tensor.matmul(m.s2[:, v % 2, f * HF:(f + 1) * HF], m.spread[:, v, :],
                                        m.duh[:, part, f * HF:(f + 1) * HF], start=part == 0, stop=part == 1)
        last.then_inc(s.dub_ps, 1)

    def total(k, g, v):
        i = TILES * b + NG * k + g
        pe.wait_ge(s.hc, i + 3)
        hc = scan_order(m.hc[v % 2], k)
        for f in range(NHF):
            if k % 2 == 0:
                rhs = hc[:, f * HF:(f + 1) * HF]
            else:
                rhs = hc.rearrange("p (w h) -> p h w", h=H)[:, f * H // 2:(f + 1) * H // 2, :]
            last = nc.tensor.matmul(m.px[0:CP, f, :], m.gather[:, v, :], rhs, start=False,
                                    stop=k == KD - 1, skip_group_check=True)
        last.then_inc(s.y_used, 1)

    for k in range(KD):
        turn = KD * b + k
        uk = scan_order(m.u[:, k % 2, :], k)
        pe.wait_ge(s.da, TILES * b + NG * k + 1)
        for f in range(NHF):
            last = nc.tensor.matmul(m.s1[0:R, f, :], m.xdtw[:, k, :], uk[:, f * HF:(f + 1) * HF],
                                    start=True, stop=True)
        last.then_inc(s.dtr_ps, 1)
        pe.wait_ge(s.bt, TILES * b + NG * k + 2)
        for o, (wt, ready) in enumerate(((m.xbw, s.brep_ps), (m.xcw, s.crep_ps))):
            for f in range(NHF):
                last = nc.tensor.matmul(m.s2[:, o, f * HF:(f + 1) * HF], wt[:, k, :],
                                        uk[:, f * HF:(f + 1) * HF], start=True, stop=True)
            last.then_inc(ready, 1)
            if o == 0:
                pe.wait_ge(s.dtr, turn + 1)
                for f in range(NHF):
                    last = nc.tensor.matmul(m.s1[0:CP, f, :], m.dtw[:, k, :], m.dtr[:, f * HF:(f + 1) * HF],
                                            start=True, stop=True)
                last.then_inc(s.dtp_ps, 1)
        pe.wait_ge(s.crep, turn + 1)
        pe.wait_ge(s.dt_split, 2 * turn + 1)
        for v in range(4):
            tile(k, v, v)
            if v >= 2:
                total(k, v - 2, v - 2)
        with pe.Fori(1, NG // 4) as q:
            for v in range(4):
                tile(k, q * 4 + v, v)
                total(k, q * 4 + v - 2, (v - 2) % 4)
        for g in (NG - 2, NG - 1):
            total(k, g, g % 4)
    pe.wait_ge(s.ysb, b + 1)
    for f in range(NHF):
        last = nc.tensor.matmul(m.s1[0:CP, f, :], m.mean[:], m.t0[:, f * HF:(f + 1) * HF], start=True, stop=True)
    last.then_inc(s.mean_ps, 1)
    pe.wait_ge(s.sq, b + 1)
    for f in range(NHF):
        last = nc.tensor.matmul(m.s2[0:CP, 0, f * HF:(f + 1) * HF], m.mean[:], m.dt[:, f * HF:(f + 1) * HF],
                                start=True, stop=True)
    last.then_inc(s.var_ps, 1)
    pe.wait_ge(s.yz, b + 1)
    for c in range(NC):
        for f in range(NHF):
            out = m.s1[0:CP, f, :] if c == 0 else m.s2[0:CP, 1, f * HF:(f + 1) * HF]
            last = nc.tensor.matmul(out, m.outw[:, c * CP:(c + 1) * CP], m.du[:, f * HF:(f + 1) * HF],
                                    start=True, stop=True)
        last.then_inc(s.out_ps, 1)


def scan_scalar(nc, act, m, b):
    s = m.s["B"]
    norm_scalar(nc, act, m, "B", b)
    act.wait_ge(s.xz_ps, 2 * b + 1)
    nc.scalar.activation(m.pad[:, 1:H + 1, 1:W + 1], m.s2[0:CP, 0, :].rearrange("p (h w) -> p h w", h=H),
                         ACT.Copy).then_inc(s.xh, 1)
    act.wait_ge(s.xz_ps, 2 * b + 2)
    nc.scalar.activation(m.z, m.s2[0:CP, 1, :], ACT.Copy)
    nc.scalar.activation(m.zs[:], m.s2[0:CP, 1, :], ACT.Exp, scale=-1.0).then_inc(s.z, 1)
    act.wait_ge(s.u_conv, b + 1)
    nc.scalar.activation(m.t1[:], m.t0[:], ACT.Exp, scale=-1.0).then_inc(s.u_exp, 1)
    s1 = m.s1[:].rearrange("p a n -> p (a n)")

    def tile(k, g, v):
        i = TILES * b + NG * k + g
        act.wait_ge(s.dtb_ps, i + 1)
        act.wait_ge(s.h, i + 1)
        nc.scalar.activation(m.da[v % 2][:], s1, ACT.Exp,
                             scale=m.arow[:, bass.ds(NG * k + g, 1)]).then_inc(s.da, 1)

    for k in range(KD):
        turn = KD * b + k
        act.wait_ge(s.dtr_ps, turn + 1)
        nc.scalar.activation(m.dtr, s1[0:R, :], ACT.Copy).then_inc(s.dtr, 1)
        act.wait_ge(s.brep_ps, turn + 1)
        nc.scalar.activation(m.brep[:], m.s2[:, 0, :], ACT.Copy).then_inc(s.brep, 1)
        act.wait_ge(s.v, turn + 1)
        nc.scalar.activation(m.t1[:], m.t1[:], ACT.Exp)
        nc.scalar.drain()
        nc.scalar.activation(m.dt[:], m.t1[:], ACT.Copy, bias=1.0)
        nc.scalar.drain()
        nc.scalar.activation(m.du[:], m.dt[:], ACT.Ln).then_inc(s.e, 1)
        act.wait_ge(s.crep_ps, turn + 1)
        nc.scalar.activation(m.crep[:], m.s2[:, 1, :], ACT.Copy).then_inc(s.crep, 1)
        with act.Fori(0, NG // 4) as q:
            for v in range(4):
                tile(k, q * 4 + v, v)
    act.wait_ge(s.var_ps, b + 1)
    nc.scalar.activation(m.t0[:], m.s2[0:CP, 0, :], ACT.Ln, bias=m.eps[:, 0:1])
    nc.scalar.drain()
    nc.scalar.activation(m.t0[:], m.t0[:], ACT.Exp, scale=-0.5).then_inc(s.rln, 1)


def scan_vector(nc, dve, m, b):
    s = m.s["B"]
    norm_vector(nc, dve, m, "B", b)
    s1 = m.s1[0:CP, :, :].rearrange("p a n -> p (a n)")
    nc.vector.memset(m.pad[:, 0, :], 0.0)
    nc.vector.memset(m.pad[:, H + 1, :], 0.0)
    nc.vector.memset(m.pad[:, 1:H + 1, 0:1], 0.0)
    nc.vector.memset(m.pad[:, 1:H + 1, W + 1:W + 2], 0.0)
    nc.vector.drain()
    dve.wait_ge(s.xh, b + 1)
    acc = m.t0[:].rearrange("p (h w) -> p h w", h=H)
    nc.vector.tensor_scalar(acc, m.pad[:, 0:H, 0:W], m.convw[:, 0:1], m.convb[:, 0:1], ALU.mult, ALU.add)
    for a in range(1, 9):
        nc.vector.drain()
        last = nc.vector.scalar_tensor_tensor(acc, m.pad[:, a // 3:a // 3 + H, a % 3:a % 3 + W],
                                              m.convw[:, a:a + 1], acc, ALU.mult, ALU.add)
    last.then_inc(s.u_conv, 1)
    dve.wait_ge(s.z, b + 1)
    nc.vector.tensor_scalar(m.zs[:], m.zs[:], 1.0, None, ALU.add)
    nc.vector.drain()
    nc.vector.reciprocal(m.zs[:], m.zs[:])
    nc.vector.drain()
    nc.vector.tensor_tensor(m.zs[:], m.zs[:], m.z, ALU.mult)
    dve.wait_ge(s.u_exp, b + 1)
    nc.vector.tensor_scalar(m.t1[:], m.t1[:], 1.0, None, ALU.add)
    nc.vector.drain()
    nc.vector.reciprocal(m.t1[:], m.t1[:])
    nc.vector.drain()
    nc.vector.tensor_tensor(m.u[:, 0, :], m.t0[:], m.t1[:], ALU.mult)
    nc.vector.drain()
    nc.vector.tensor_copy(m.u[:, 1, :].rearrange("p (w h) -> p w h", h=H),
                          m.u[:, 0, :].rearrange("p (h w) -> p w h", h=H)).then_inc(s.u, 1)

    def tile(k, g, v):
        i = TILES * b + NG * k + g
        dve.wait_ge(s.dub_ps, i + 1)
        nc.vector.tensor_tensor(m.bt[v % 2][:], m.s2[:, v % 2, :], m.brep[:], ALU.mult).then_inc(s.bt, 1)
        nc.vector.drain()
        dve.wait_ge(s.da, i + 2)
        dve.wait_ge(s.hc, i + 1)
        nc.vector.tensor_tensor_scan(m.hs[v % 2][:], m.da[v % 2][:], m.bt[v % 2][:], 0.0,
                                     ALU.mult, ALU.add).then_inc(s.h, 1)

    for k in range(KD):
        turn = KD * b + k
        dve.wait_ge(s.dtp_ps, turn + 1)
        nc.vector.tensor_scalar(m.t0[:], s1, m.dtb[:, k:k + 1], None, ALU.add)
        nc.vector.drain()
        nc.vector.scalar_tensor_tensor(m.t1[:], m.t0[:], -1.0, m.t0[:], ALU.mult, ALU.min).then_inc(s.v, 1)
        dve.wait_ge(s.e, turn + 1)
        nc.vector.scalar_tensor_tensor(m.dt[:], m.dt[:], 1.0, m.t1[:], ALU.subtract, ALU.subtract)
        nc.vector.drain()
        nc.vector.tensor_tensor(m.du[:], m.du[:], m.dt[:], ALU.subtract)
        nc.vector.drain()
        nc.vector.scalar_tensor_tensor(m.du[:], m.t1[:], 0.5, m.du[:], ALU.mult, ALU.max)
        nc.vector.drain()
        nc.vector.scalar_tensor_tensor(m.dt[:], m.t0[:], 0.0, m.du[:], ALU.max, ALU.add)
        nc.vector.drain()
        nc.vector.tensor_copy(m.dth[:, 0, :], m.dt[:])
        nc.vector.drain()
        nc.vector.tensor_tensor(m.dth[:, 1, :], m.dt[:], m.dth[:, 0, :].bitcast(F32), ALU.subtract) \
            .then_inc(s.dt_split, 1)
        nc.vector.tensor_tensor(m.du[:], m.dt[:], scan_order(m.u[:, k % 2, :], k), ALU.mult)
        nc.vector.drain()
        nc.vector.tensor_copy(m.duh[:, 0, :], m.du[:])
        nc.vector.drain()
        nc.vector.tensor_tensor(m.duh[:, 1, :], m.du[:], m.duh[:, 0, :].bitcast(F32), ALU.subtract) \
            .then_inc(s.dt_split, 1)
        dve.wait_ge(s.brep, turn + 1)
        settle(dve, m)
        with dve.Fori(0, NG // 4) as q:
            for v in range(4):
                tile(k, q * 4 + v, v)
    dve.wait_ge(s.y_used, TILES * b + TILES + 4)
    nc.vector.tensor_copy(m.t0[:], m.px[0:CP, :, :].rearrange("p a n -> p (a n)")).then_inc(s.ysb, 1)
    nc.vector.drain()
    dve.wait_ge(s.mean_ps, b + 1)
    nc.vector.tensor_tensor(m.t1[:], m.t0[:], s1, ALU.subtract)
    nc.vector.drain()
    nc.vector.tensor_tensor(m.dt[:], m.t1[:], m.t1[:], ALU.mult).then_inc(s.sq, 1)
    dve.wait_ge(s.rln, b + 1)
    nc.vector.tensor_tensor(m.t1[:], m.t1[:], m.t0[:], ALU.mult)
    nc.vector.drain()
    nc.vector.tensor_scalar(m.t1[:], m.t1[:], m.lng[:, 0:1], m.lnb[:, 0:1], ALU.mult, ALU.add)
    nc.vector.drain()
    nc.vector.tensor_tensor(m.du[:], m.t1[:], m.zs[:], ALU.mult).then_inc(s.yz, 1)
    for c in range(NC):
        dve.wait_ge(s.out_ps, NC * b + c + 1)
        psum = s1 if c == 0 else m.s2[0:CP, 1, :]
        nc.vector.tensor_tensor(m.x[:, c, :], psum, m.x[:, c, :], ALU.add).then_inc(s.x_done, 1)
    nc.vector.drain()


def place_selectors(nc, pool, m, i, g, v):
    s = m.s["B"]
    pool.wait_ge(s.y_used, i + 1)
    nc.gpsimd.tensor_copy(m.gather[:, v, :], m.gather_t[:, bass.ds(g, 1), :].rearrange("p a n -> p (a n)"))
    nc.gpsimd.tensor_copy(m.spread[:, v, :], m.spread_t[:, bass.ds(g, 1), :].rearrange("p a n -> p (a n)")
                          .bitcast(F32)).then_inc(s.sel, 1)


def attn_pool(nc, pool, m, L, b):
    s = m.s[L]
    pool.wait_ge(s.v_used, 4 * b + 4)
    settle(pool, m)

    def body(j, u, ahead):
        h = j * NBUF + u
        pool.wait_ge(s.pt_used, NH * NT * b + NT * h + 1)
        settle(pool, m)
        nc.gpsimd.tensor_copy(m.vh[u][:, :, 0:HD], m.v[:, :, bass.ds(h, 1), :].rearrange("p t a d -> p t (a d)")) \
            .then_inc(s.vh, 1)

    heads_loop(pool, body)


def scan_pool(nc, pool, m, b):
    s = m.s["B"]
    for k in range(KD):
        pool.wait_ge(s.crep, KD * b + k + 1)
        settle(pool, m)
        with pool.Fori(0, NG // 4) as q:
            for v in range(4):
                i = TILES * b + NG * k + q * 4 + v
                place_selectors(nc, pool, m, i + 2, q * 4 + v + 2, (v + 2) % 4)
                pool.wait_ge(s.h, i + 3)
                pool.wait_ge(s.y_used, i + 3)
                nc.gpsimd.tensor_tensor(m.hc[v % 2][:], m.hs[v % 2][:], m.crep[:], ALU.mult).then_inc(s.hc, 1)



def build(nc, d, out):
    ctx = ExitStack()
    nc.disable_value_cache = True
    with ctx:
        m = allocate(nc, ctx)
        block = ctx.enter_context(nc.Block())

        @block.sync
        def _(sp):
            loads = [(m.ident[:], d["ident"]), (m.group[:], d["group"]), (m.mean[:], d["mean"]),
                     (m.rot[:], d["rot"]),
                     (m.hot_in[:], d["onehot"]), (m.window_in[64:P, :], d["window"]),
                     (m.lorows[:], d["lorows"]), (m.gather_t[:], d["gather"]),
                     (m.spread_in[:], d["spread"]),
                     (m.inw[:], d["in_w"]), (m.outw[:], d["out_w"]), (m.convw[:], d["conv_w"]),
                     (m.convb[:], d["conv_b"]), (m.xdtw[:], d["xdt_w"]), (m.xbw[:], d["xb_w"]),
                     (m.xcw[:], d["xc_w"]), (m.dtw[:], d["dt_w"]), (m.dtb[:], d["dt_b"]),
                     (m.arow[:], d["a_log"]), (m.dskip[:], d["d_skip"]), (m.lng[:], d["ln_g"]),
                     (m.lnb[:], d["ln_b"])]
            for L in ATTN:
                loads += [(m.w[L].qkv[:], d[f"qkv_w{L}"]), (m.w[L].proj[:], d[f"proj_w{L}"])]
                if L in BIASED:
                    vb = d[f"qkv_b{L}"]
                    loads += [(m.w[L].qkb[:], d[f"qk_b{L}"]), (m.w[L].pb[:], d[f"proj_b{L}"]),
                              (m.w[L].vb[:].rearrange("p a h d -> p a (h d)"),
                               bass.AP(vb.tensor, 2 * C, [[0, P], [0, 2], [1, C]]))]
            for i in range(2):
                loads += [(m.rel_in[i][r * HD:(r + 1) * HD], d[("rel_h", "rel_w")[i]]) for r in range(3)]
            for dst, src in loads:
                sp.dma_start(dst, src).then_inc(m.const_in, 16)
            assert len(loads) == CONSTANTS
            sp.wait_ge(m.a_log, 1)
            sp.dma_start(m.zero, m.zeros[:]).then_inc(m.zero_in, 16)
            sp.wait_ge(m.const_ready, 1)
            sp.wait_ge(m.zero_in, 16)
            with sp.Fori(0, B) as b:
                sp.dma_start(m.x[:], d["x"][bass.ds(b, 1)].rearrange("a c p n -> p (a c) n")) \
                    .then_inc(m.x_in, 16)
                sp.dma_start(m.cos[:], d["cos"]).then_inc(m.rope_in, 16)
                sp.dma_start(m.sin[:], d["sin"]).then_inc(m.rope_in, 16)
                for L in ATTN:
                    attn_sync(nc, sp, m, L, b)
                sp.wait_ge(m.s["D"].x_done, NC * b + NC)
                sp.dma_start(out[bass.ds(b, 1)].rearrange("a c p n -> p (a c) n"), m.x[:]) \
                    .then_inc(m.out_done, 16)
                sp.wait_ge(m.out_done, 16 * b + 16)
                settle(sp, m)

        @block.vector
        def _(dve):
            nc.vector.memset(m.zeros[:], 0.0).then_inc(m.a_log, 1)
            nc.vector.memset(m.eps[:], 1e-5)
            nc.vector.memset(m.den[:], 1.0)
            for u in range(NBUF):
                nc.vector.memset(m.vh[u][:, :, HD:32], 0.0)
                nc.vector.memset(m.vh[u][:, :, 32:VC], 1.0)
                nc.vector.memset(m.kb[u][BR:BR + MB, :], 1.0)
                nc.vector.memset(m.qs[u][32:64, :].bitcast(F32), 0.0)
                nc.vector.memset(m.ks[u][32:64, :].bitcast(F32), 1.0)
            dve.wait_ge(m.const_in, 16 * CONSTANTS)
            nc.vector.tensor_scalar(m.arow[:], m.arow[:], A_LOG_MAX, None, ALU.min).then_inc(m.a_log, 1)
            nc.vector.tensor_copy(m.hot[:], m.hot_in[:])
            for u in range(NBUF):
                nc.vector.tensor_copy(m.qs[u][64:P, :], m.window_in[64:P, :])
                nc.vector.tensor_copy(m.ks[u][64:P, :], m.hot_in[64:P, :])
            nc.vector.tensor_copy(m.spread_t[:], m.spread_in[:])
            nc.vector.tensor_scalar(m.w["C"].qkb[:, 2:4], m.w["C"].qkb[:, 2:4], HD ** -0.5, None, ALU.mult)
            nc.vector.tensor_reduce(m.gt[:, 0:1], m.dskip[:], AX.X, ALU.add)
            nc.vector.drain()
            nc.vector.tensor_scalar(m.diag[:], m.ident[0:CP, 0:CP], m.gt[:, 0:1], None, ALU.mult)
            dve.wait_ge(m.a_exp, 1)
            nc.vector.tensor_scalar(m.arow[:], m.arow[:], -1.0, None, ALU.mult)
            for i, rel in enumerate((m.relh, m.relw)):
                v = m.rel_in[i][:]
                nc.vector.tensor_copy(rel[:], v)
                nc.vector.drain()
                nc.vector.scalar_tensor_tensor(rel[:], rel[:].bitcast(F32), m.lorows[:, 0:1], v,
                                               ALU.mult, ALU.add)
            nc.vector.drain().then_inc(m.const_ready, 1)
            with dve.Fori(0, B) as b:
                dve.wait_ge(m.x_in, 16 * b + 16)
                attn_vector(nc, dve, m, "A", b)
                scan_vector(nc, dve, m, b)
                attn_vector(nc, dve, m, "C", b)
                attn_vector(nc, dve, m, "D", b)

        @block.scalar
        def _(act):
            for L in ATTN:
                act.sem_inc(m.s[L].pt, 2)
            act.sem_inc(m.s["B"].da, 1)
            act.wait_ge(m.a_log, 2)
            nc.scalar.activation(m.arow[:], m.arow[:], ACT.Exp).then_inc(m.a_exp, 1)
            act.wait_ge(m.const_ready, 1)
            with act.Fori(0, B) as b:
                attn_scalar(nc, act, m, "A", b)
                scan_scalar(nc, act, m, b)
                attn_scalar(nc, act, m, "C", b)
                attn_scalar(nc, act, m, "D", b)

        @block.tensor
        def _(pe):
            for L in ATTN:
                pe.sem_inc(m.s[L].pt_used, 4)
                pe.sem_inc(m.s[L].mx_used, 1)
                pe.sem_inc(m.s[L].o_used, 1)
                pe.sem_inc(m.s[L].sums, 1)
                pe.sem_inc(m.s[L].o, 1)
                for u in range(NBUF):
                    pe.sem_inc(m.s[L].o_out[u], 16)
            pe.sem_inc(m.s["B"].bt, 2)
            pe.sem_inc(m.s["B"].h, 2)
            pe.sem_inc(m.s["B"].y_used, 4)
            pe.wait_ge(m.const_ready, 1)
            with pe.Fori(0, B) as b:
                attn_tensor(nc, pe, m, "A", b)
                scan_tensor(nc, pe, m, b)
                attn_tensor(nc, pe, m, "C", b)
                attn_tensor(nc, pe, m, "D", b)

        @block.gpsimd
        def _(pool):
            pool.sem_inc(m.s["B"].hc, 2)
            pool.wait_ge(m.const_ready, 1)
            for g in range(2):
                place_selectors(nc, pool, m, g, g, g)
            with pool.Fori(0, B) as b:
                attn_pool(nc, pool, m, "A", b)
                scan_pool(nc, pool, m, b)
                attn_pool(nc, pool, m, "C", b)
                attn_pool(nc, pool, m, "D", b)



def chunks(a):
    return a.reshape(NC, CP, -1).transpose(1, 0, 2)


def layout(i):
    d = dict(constants())
    d["x"] = i["x"].reshape(B, N, NC, CP).transpose(0, 2, 3, 1)
    rope = i["L0_conv_rope"].reshape(N, 2, HD).transpose(1, 2, 0)
    d["sin"], d["cos"] = np.tile(rope[0], (CP // HD, 1)), np.tile(rope[1], (CP // HD, 1))
    d["qkv_wA"], d["proj_wA"] = chunks(i["L0_conv_qkv_w"]), chunks(i["L0_conv_proj_w"])
    d["qkv_wC"], d["proj_wC"] = chunks(i["L2_conv_qkv_w"].T), chunks(i["L2_conv_proj_w"].T)
    d["qkv_wD"], d["proj_wD"] = chunks(i["L3_conv_w_qkv"]), chunks(i["L3_conv_w_out"])
    for L, n in (("A", "L0"), ("C", "L2")):
        qkv_b = i[f"{n}_conv_qkv_b"]
        d[f"qkv_b{L}"] = qkv_b
        d[f"qk_b{L}"] = qkv_b[0:2 * C].reshape(4, CP).T
        d[f"proj_b{L}"] = i[f"{n}_conv_proj_b"].reshape(NC, CP).T
    at = np.arange(H)[:, None] - np.arange(H)[None, :] + H - 1
    for n in ("h", "w"):
        table = i[f"L2_conv_rel_pos_{n}"]
        d[f"rel_{n}"] = table[np.minimum(at, table.shape[0] - 1)].transpose(2, 0, 1)
    d["in_w"] = chunks(i["L1_conv_in_proj_w"].T)
    d["out_w"] = i["L1_conv_out_proj_w"].T
    d["conv_w"] = i["L1_conv_conv_w"].reshape(CP, 9)
    d["conv_b"] = i["L1_conv_conv_b"].reshape(CP, 1)
    xp = i["L1_conv_x_proj_w"].transpose(2, 0, 1)
    d["xdt_w"] = xp[:, :, 0:R]
    d["xb_w"] = np.tile(xp[:, :, R:R + NS], (1, 1, DB))
    d["xc_w"] = np.tile(xp[:, :, R + NS:R + 2 * NS], (1, 1, DB))
    d["dt_w"] = i["L1_conv_dt_projs_w"].transpose(2, 0, 1)
    d["dt_b"] = i["L1_conv_dt_projs_b"].T
    d["a_log"] = i["L1_conv_A_logs"].reshape(KD, NG, DB, NS).transpose(2, 3, 0, 1).reshape(P, KD * NG)
    d["d_skip"] = i["L1_conv_Ds"].reshape(KD, CP).T
    d["ln_g"] = i["L1_conv_out_norm_g"].reshape(CP, 1)
    d["ln_b"] = i["L1_conv_out_norm_b"].reshape(CP, 1)
    return {k: np.ascontiguousarray(v) for k, v in d.items()}


def kernel(**inputs):
    import concourse.bacc as bacc
    from concourse.bass_utils import run_bass_kernel_spmd as run

    arrays = layout({k: np.asarray(v) for k, v in inputs.items()})
    nc = bacc.Bacc("TRN2", target_bir_lowering=False, num_devices=1)
    d = {k: nc.dram_tensor(f"in_{k}", a.shape, mybir.dt.from_np(a.dtype), kind="ExternalInput").ap()
         for k, a in arrays.items()}
    out = nc.dram_tensor("out", (B, NC, CP, N), F32, kind="ExternalOutput").ap()
    build(nc, d, out)
    r = run(nc, [{f"in_{k}": a for k, a in arrays.items()}], core_ids=[0])
    return r.results[0]["out"].transpose(0, 3, 1, 2).reshape(B, H, W, C)
```
